# Optimizing a Trainium2 kernel written in Bass

```python
import numpy as np
import jax
import jax.numpy as jnp

def _softmax(x, axis=-1):
    return jax.nn.softmax(x, axis=axis)

def _gelu(x):
    return jax.nn.gelu(x, approximate=True)

def _silu(x):
    return jax.nn.silu(x)

def _sigmoid(x):
    return jax.nn.sigmoid(x)

def _layernorm(x, axis=-1, eps=1e-05):
    m = jnp.mean(x, axis=axis, keepdims=True)
    v = jnp.var(x, axis=axis, keepdims=True)
    return (x - m) / jnp.sqrt(v + eps)

def _scatter_add(tgt, idx, src, axis=0):
    return tgt.at[idx].add(src)

def _segment_sum(src, seg, n):
    return jax.ops.segment_sum(src, seg, n)
kernel_name = 'mk_gnn_preln_d2_gnn_r8_4c0f3e'

def setup_inputs(seed: int=0):
    np.random.seed(seed)
    _w = jnp.asarray

    def _rec_inputs():
        import jax
        import jax.numpy as jnp
        _gk = jax.random.key(seed)
        x = -0.0005121 + 1.001 * jax.random.normal(jax.random.fold_in(_gk, 1), (12500, 160), jnp.float32)
        _s = jax.random.randint(jax.random.fold_in(_gk, 2), (100000,), 0, 12500, jnp.int32)
        _d = jax.random.randint(jax.random.fold_in(_gk, 3), (100000,), 0, 12500, jnp.int32)
        _loop = jnp.arange(12500, dtype=jnp.int32)
        src = jnp.concatenate([_s, _d, _loop])
        dst = jnp.concatenate([_d, _s, _loop])
        _o = jnp.argsort(dst, stable=True)
        src = src[_o]
        dst = dst[_o]
        edge_attr_16 = -0.000191324 + 0.999809 * jax.random.normal(jax.random.fold_in(_gk, 12), (212500, 16), jnp.float32)
        edge_attr_3 = 0.00047201 + 1.00023 * jax.random.normal(jax.random.fold_in(_gk, 13), (212500, 3), jnp.float32)
        edge_attr_4 = 0.000126197 + 0.999763 * jax.random.normal(jax.random.fold_in(_gk, 14), (212500, 4), jnp.float32)
        edge_attr_64 = 0.000279952 + 1.00013 * jax.random.normal(jax.random.fold_in(_gk, 15), (212500, 64), jnp.float32)
        node_vec1 = jax.random.uniform(jax.random.fold_in(_gk, 17), (12500, 1), jnp.float32, 0.0, 1)
        return (x, src, dst, edge_attr_16, edge_attr_3, edge_attr_4, edge_attr_64, node_vec1)
    x, src, dst, edge_attr_16, edge_attr_3, edge_attr_4, edge_attr_64, node_vec1 = _rec_inputs()

    def _L0_gnn_setup():
        import jax, jax.numpy as jnp
        import numpy as np
        N = 2500
        E = 40000
        MUL0 = 64
        MUL1 = 32
        FC_IN = 16
        FC_H = 64
        WNUM = 192
        key = jax.random.key(seed)
        ks = jax.random.split(key, 16)
        return {'x': jax.random.normal(ks[0], (N, MUL0 + 3 * MUL1), jnp.float32), 'node_attr': jnp.ones((N, 1), jnp.float32), 'edge_scalars': jax.random.normal(ks[1], (E, FC_IN), jnp.float32), 'edge_attr_sh': jax.random.normal(ks[2], (E, 4), jnp.float32), 'edge_src': jax.random.randint(ks[3], (E,), 0, N), 'edge_dst': jax.random.randint(ks[4], (E,), 0, N), 'Wfc1': jax.random.normal(ks[5], (FC_IN, FC_H), jnp.float32), 'Wfc2': jax.random.normal(ks[6], (FC_H, WNUM), jnp.float32), 'Wsc0': jax.random.normal(ks[7], (MUL0, MUL0), jnp.float32), 'Wsc1': jax.random.normal(ks[8], (MUL1, MUL1), jnp.float32), 'Wl1_0': jax.random.normal(ks[9], (MUL0, MUL0), jnp.float32), 'Wl1_1': jax.random.normal(ks[10], (MUL1, MUL1), jnp.float32), 'Wl2_s': jax.random.normal(ks[11], (MUL0 + MUL1, MUL0), jnp.float32), 'Wl2_v': jax.random.normal(ks[12], (MUL0 + MUL1, MUL1), jnp.float32), 'Wa': 0.1 * jax.random.normal(ks[13], (MUL0 + MUL1, 1), jnp.float32)}
    _L0_gnn_all = _L0_gnn_setup()
    _L0_gnn_in = {k: v for k, v in _L0_gnn_all.items() if k in ('Wfc1', 'Wfc2', 'Wsc0', 'Wsc1', 'Wl1_0', 'Wl1_1', 'Wl2_s', 'Wl2_v', 'Wa')}
    del _L0_gnn_all

    def _L1_gnn_setup():
        import jax, jax.numpy as jnp
        import numpy as np
        N_NODES = 1250
        N_EDGES = 40000
        MUL0, MUL1 = (64, 32)
        EDGE_DIM = 64
        W_NUMEL = 224
        DENOM = 32.0
        SQRT3 = 3.0 ** 0.5
        INV_SQRT3 = 1.0 / SQRT3
        INV_SQRT2 = 2.0 ** (-0.5)

        def _forward(node_feature, edge_attr, edge_feature, W_skip0, W_skip1, W_nl0, W_nl1, W_fc1, W_fc2, W_out_s, W_out_v, edge_index):
            N = node_feature.shape[0]
            E = edge_attr.shape[0]
            s = node_feature[:, :MUL0]
            v = node_feature[:, MUL0:].reshape(N, MUL1, 3)
            skip_s = s @ W_skip0
            skip_v = jnp.einsum('nmi,mk->nki', v, W_skip1)
            s = s @ W_nl0
            v = jnp.einsum('nmi,mk->nki', v, W_nl1)
            rhat = edge_attr / jnp.linalg.norm(edge_attr, axis=-1, keepdims=True)
            sh1 = SQRT3 * rhat
            w = jax.nn.relu(edge_feature @ W_fc1) @ W_fc2
            w0, w1, w2, w3, w4 = jnp.split(w, [64, 128, 160, 192], axis=-1)
            src, dst = (edge_index[0], edge_index[1])
            xs = s[dst]
            xv = v[dst]
            out0a = w0 * xs
            out0b = w3 * (jnp.einsum('emi,ei->em', xv, sh1) * INV_SQRT3)
            out1a = (w1 * xs)[:, :, None] * sh1[:, None, :]
            out1b = w2[:, :, None] * xv
            out1c = w4[:, :, None] * (jnp.cross(xv, sh1[:, None, :]) * INV_SQRT2)
            tp = jnp.concatenate([out0a, out0b, out1a.reshape(E, -1), out1b.reshape(E, -1), out1c.reshape(E, -1)], axis=-1)
            agg = jax.ops.segment_sum(tp, src, num_segments=N) / DENOM
            agg_s = agg[:, :96]
            agg_v = agg[:, 96:].reshape(N, 128, 3)
            out_s = agg_s @ W_out_s + skip_s
            out_v = jnp.einsum('nmi,mk->nki', agg_v, W_out_v) + skip_v
            fs = jax.nn.silu(out_s[:, :MUL0])
            gate = jax.nn.sigmoid(out_s[:, MUL0:MUL0 + 32])
            gv = gate[:, :, None] * out_v
            return jnp.concatenate([fs, gv.reshape(N, -1)], axis=-1)
        key = jax.random.key(seed)
        ks = jax.random.split(key, 12)

        def lin(k, fi, fo):
            return jax.random.normal(k, (fi, fo), jnp.float32) / np.float32(np.sqrt(fi))
        return {'node_feature': jax.random.normal(ks[0], (N_NODES, MUL0 + 3 * MUL1), jnp.float32), 'edge_attr': jax.random.normal(ks[1], (N_EDGES, 3), jnp.float32), 'edge_feature': jax.random.normal(ks[2], (N_EDGES, EDGE_DIM), jnp.float32), 'W_skip0': lin(ks[3], MUL0, 96), 'W_skip1': lin(ks[4], MUL1, 32), 'W_nl0': lin(ks[5], MUL0, MUL0), 'W_nl1': lin(ks[6], MUL1, MUL1), 'W_fc1': lin(ks[7], EDGE_DIM, 64), 'W_fc2': lin(ks[8], 64, W_NUMEL), 'W_out_s': lin(ks[9], 96, 96), 'W_out_v': lin(ks[10], 128, 32), 'edge_index': jax.random.randint(ks[11], (2, N_EDGES), 0, N_NODES)}
    _L1_gnn_all = _L1_gnn_setup()
    _L1_gnn_in = {k: v for k, v in _L1_gnn_all.items() if k in ('W_skip0', 'W_skip1', 'W_nl0', 'W_nl1', 'W_fc1', 'W_fc2', 'W_out_s', 'W_out_v')}
    del _L1_gnn_all
    return {'x': x, 'src': src, 'dst': dst, 'edge_attr_16': edge_attr_16, 'edge_attr_3': edge_attr_3, 'edge_attr_4': edge_attr_4, 'edge_attr_64': edge_attr_64, 'node_vec1': node_vec1, 'L0_gnn_Wfc1': _L0_gnn_in['Wfc1'], 'L0_gnn_Wfc2': _L0_gnn_in['Wfc2'], 'L0_gnn_Wsc0': _L0_gnn_in['Wsc0'], 'L0_gnn_Wsc1': _L0_gnn_in['Wsc1'], 'L0_gnn_Wl1_0': _L0_gnn_in['Wl1_0'], 'L0_gnn_Wl1_1': _L0_gnn_in['Wl1_1'], 'L0_gnn_Wl2_s': _L0_gnn_in['Wl2_s'], 'L0_gnn_Wl2_v': _L0_gnn_in['Wl2_v'], 'L0_gnn_Wa': _L0_gnn_in['Wa'], 'L1_gnn_W_skip0': _L1_gnn_in['W_skip0'], 'L1_gnn_W_skip1': _L1_gnn_in['W_skip1'], 'L1_gnn_W_nl0': _L1_gnn_in['W_nl0'], 'L1_gnn_W_nl1': _L1_gnn_in['W_nl1'], 'L1_gnn_W_fc1': _L1_gnn_in['W_fc1'], 'L1_gnn_W_fc2': _L1_gnn_in['W_fc2'], 'L1_gnn_W_out_s': _L1_gnn_in['W_out_s'], 'L1_gnn_W_out_v': _L1_gnn_in['W_out_v']}

def reference(x, src, dst, edge_attr_16, edge_attr_3, edge_attr_4, edge_attr_64, node_vec1, L0_gnn_Wfc1, L0_gnn_Wfc2, L0_gnn_Wsc0, L0_gnn_Wsc1, L0_gnn_Wl1_0, L0_gnn_Wl1_1, L0_gnn_Wl2_s, L0_gnn_Wl2_v, L0_gnn_Wa, L1_gnn_W_skip0, L1_gnn_W_skip1, L1_gnn_W_nl0, L1_gnn_W_nl1, L1_gnn_W_fc1, L1_gnn_W_fc2, L1_gnn_W_out_s, L1_gnn_W_out_v):
    import jax
    import jax.numpy as jnp

    def _L0_gnn_ref(x, node_attr, edge_scalars, edge_attr_sh, edge_src, edge_dst, Wfc1, Wfc2, Wsc0, Wsc1, Wl1_0, Wl1_1, Wl2_s, Wl2_v, Wa):
        import jax, jax.numpy as jnp
        import numpy as np
        N = 2500
        E = 40000
        MUL0 = 64
        MUL1 = 32
        FC_IN = 16
        FC_H = 64
        WNUM = 192
        n = x.shape[0]
        x0 = x[:, :MUL0]
        x1 = x[:, MUL0:].reshape(n, MUL1, 3)
        a = node_attr
        h = jax.nn.silu(edge_scalars @ (Wfc1 / jnp.sqrt(jnp.float32(FC_IN))))
        w = h @ (Wfc2 / jnp.sqrt(jnp.float32(FC_H)))
        w0 = w[:, :64]
        w1 = w[:, 64:128]
        w2 = w[:, 128:160]
        w3 = w[:, 160:192]
        inv8 = 1.0 / jnp.sqrt(jnp.float32(MUL0))
        inv32 = 1.0 / jnp.sqrt(jnp.float32(MUL1))
        sc = jnp.concatenate([x0 @ Wsc0 * a * inv8, (jnp.einsum('num,uv->nvm', x1, Wsc1) * a[..., None] * inv32).reshape(n, 3 * MUL1)], axis=1)
        f0 = x0 @ Wl1_0 * a * inv8
        f1 = jnp.einsum('num,uv->nvm', x1, Wl1_1) * a[..., None] * inv32
        e0 = f0[edge_src]
        e1 = f1[edge_src]
        sh0 = edge_attr_sh[:, :1]
        sh1 = edge_attr_sh[:, 1:4]
        mid0 = w0 * e0 * sh0
        mid1 = w3 * jnp.einsum('eum,em->eu', e1, sh1) / jnp.sqrt(3.0)
        mid2 = w1[:, :, None] * e0[:, :, None] * sh1[:, None, :]
        mid3 = w2[:, :, None] * e1 * sh0[:, :, None]
        cnt = jnp.clip(jax.ops.segment_sum(jnp.ones(edge_dst.shape, x.dtype), edge_dst, num_segments=n), 1.0)

        def smean(v):
            s = jax.ops.segment_sum(v, edge_dst, num_segments=n)
            return s / cnt.reshape((n,) + (1,) * (v.ndim - 1))
        n0, n1 = (smean(mid0), smean(mid1))
        n2, n3 = (smean(mid2), smean(mid3))
        scal = jnp.concatenate([n0, n1], axis=1)
        vec = jnp.concatenate([n2, n3], axis=1)
        inv96 = 1.0 / jnp.sqrt(jnp.float32(MUL0 + MUL1))
        alpha = scal @ Wa * a * inv96
        out_s = scal @ Wl2_s * a * inv96
        out_v = jnp.einsum('num,uv->nvm', vec, Wl2_v) * a[..., None] * inv96
        conv = jnp.concatenate([out_s, out_v.reshape(n, 3 * MUL1)], axis=1)
        return sc + alpha * conv

    def _L1_gnn_ref(node_feature, edge_attr, edge_feature, W_skip0, W_skip1, W_nl0, W_nl1, W_fc1, W_fc2, W_out_s, W_out_v, edge_index):
        import jax, jax.numpy as jnp
        import numpy as np
        N_NODES = 1250
        N_EDGES = 40000
        MUL0, MUL1 = (64, 32)
        EDGE_DIM = 64
        W_NUMEL = 224
        DENOM = 32.0
        SQRT3 = 3.0 ** 0.5
        INV_SQRT3 = 1.0 / SQRT3
        INV_SQRT2 = 2.0 ** (-0.5)

        def _forward(node_feature, edge_attr, edge_feature, W_skip0, W_skip1, W_nl0, W_nl1, W_fc1, W_fc2, W_out_s, W_out_v, edge_index):
            N = node_feature.shape[0]
            E = edge_attr.shape[0]
            s = node_feature[:, :MUL0]
            v = node_feature[:, MUL0:].reshape(N, MUL1, 3)
            skip_s = s @ W_skip0
            skip_v = jnp.einsum('nmi,mk->nki', v, W_skip1)
            s = s @ W_nl0
            v = jnp.einsum('nmi,mk->nki', v, W_nl1)
            rhat = edge_attr / jnp.linalg.norm(edge_attr, axis=-1, keepdims=True)
            sh1 = SQRT3 * rhat
            w = jax.nn.relu(edge_feature @ W_fc1) @ W_fc2
            w0, w1, w2, w3, w4 = jnp.split(w, [64, 128, 160, 192], axis=-1)
            src, dst = (edge_index[0], edge_index[1])
            xs = s[dst]
            xv = v[dst]
            out0a = w0 * xs
            out0b = w3 * (jnp.einsum('emi,ei->em', xv, sh1) * INV_SQRT3)
            out1a = (w1 * xs)[:, :, None] * sh1[:, None, :]
            out1b = w2[:, :, None] * xv
            out1c = w4[:, :, None] * (jnp.cross(xv, sh1[:, None, :]) * INV_SQRT2)
            tp = jnp.concatenate([out0a, out0b, out1a.reshape(E, -1), out1b.reshape(E, -1), out1c.reshape(E, -1)], axis=-1)
            agg = jax.ops.segment_sum(tp, src, num_segments=N) / DENOM
            agg_s = agg[:, :96]
            agg_v = agg[:, 96:].reshape(N, 128, 3)
            out_s = agg_s @ W_out_s + skip_s
            out_v = jnp.einsum('nmi,mk->nki', agg_v, W_out_v) + skip_v
            fs = jax.nn.silu(out_s[:, :MUL0])
            gate = jax.nn.sigmoid(out_s[:, MUL0:MUL0 + 32])
            gv = gate[:, :, None] * out_v
            return jnp.concatenate([fs, gv.reshape(N, -1)], axis=-1)
        return _forward(node_feature, edge_attr, edge_feature, W_skip0, W_skip1, W_nl0, W_nl1, W_fc1, W_fc2, W_out_s, W_out_v, edge_index)
    edge_index = jnp.stack([src, dst])
    h = jnp.maximum(_layernorm(x, axis=-1), 0.0)
    x = x + _L0_gnn_ref(h, node_vec1, edge_attr_16, edge_attr_4, src, dst, L0_gnn_Wfc1, L0_gnn_Wfc2, L0_gnn_Wsc0, L0_gnn_Wsc1, L0_gnn_Wl1_0, L0_gnn_Wl1_1, L0_gnn_Wl2_s, L0_gnn_Wl2_v, L0_gnn_Wa)
    h = jnp.maximum(_layernorm(x, axis=-1), 0.0)
    x = x + _L1_gnn_ref(h, edge_attr_3, edge_attr_64, L1_gnn_W_skip0, L1_gnn_W_skip1, L1_gnn_W_nl0, L1_gnn_W_nl1, L1_gnn_W_fc1, L1_gnn_W_fc2, L1_gnn_W_out_s, L1_gnn_W_out_v, edge_index)
    return x

_drawn_inputs = setup_inputs


def setup_inputs(seed=0):
    import zlib

    import numpy as np

    out = dict(_drawn_inputs(seed))
    spreads = {}
    factors = {}
    for name, (base, spread) in spreads.items():
        noise = np.random.default_rng([zlib.crc32(name.encode()), seed]).standard_normal(out[name].shape)
        drawn = base * np.exp(spread * noise) if base else spread * noise
        out[name] = jnp.asarray(drawn.astype(out[name].dtype))
    for name, factor in factors.items():
        out[name] = (out[name] * factor).astype(out[name].dtype)
    return out
```

```python
from contextlib import ExitStack

import numpy as np

import concourse.bass as bass
from concourse import mybir

F32 = mybir.dt.float32
BF16 = mybir.dt.bfloat16
I32 = mybir.dt.int32
ALU = mybir.AluOpType
ACT = mybir.ActivationFunctionType
AX = mybir.AxisListType

P = 128
N_NODES = 12500
N_EDGES = 212500
NBLK = -(-N_NODES // P)
SPARE = NBLK
N_PAD = NBLK * P
N_TAB = (NBLK + 1) * P
CHUNK_TILES = 8
CHUNK = CHUNK_TILES * P
NCHUNK = -(-N_EDGES // CHUNK)
E_PAD = NCHUNK * CHUNK
NCOL = NCHUNK * CHUNK_TILES
NBIN = 100
ST_TILES = 2
ST = ST_TILES * P
ST_SHIFT = 8
assert 1 << ST_SHIFT == ST
SLOTS = 4
NST = -(-(N_EDGES // ST + NBLK) // SLOTS) * SLOTS
HST = NST // 2
assert E_PAD - N_EDGES >= ST and NST <= 1024 and N_TAB > N_PAD

S0, V0 = 64, 96
D = S0 + V0
SQRT3 = 3.0 ** 0.5
DENOM = 32.0
LN_EPS = 1e-5


class Layer:
    pass


L0 = Layer()
L0.n = 0
L0.fc_in, L0.ea, L0.width = 16, 20, 24
L0.sh_at, L0.nsh = 16, 4
L0.key_at, L0.idx_at = 21, 20
L0.wnum = 192
L0.skip_cols = (64, 96)
L0.agg = 449
L0.banks = [449]
L0.pw = 320
L0.sums = [(1, 0, (1, 160, 160), 0), (2, 160, (1, 96, 96), 160),
           (3, 160, (1, 64, 64), 256), (3, 256, (1, 32, 32), 320),
           (4, 160, (1, 64, 64), 352), (4, 288, (1, 32, 32), 416)]
L0.nhot = 5
L0.out_cols = 161
L0.kchunks = [128, 128, 128, 64]

L1 = Layer()
L1.n = 1
L1.fc_in, L1.ea, L1.width = 64, 67, 69
L1.sh_at, L1.nsh = 64, 3
L1.key_at, L1.idx_at = 67, 68
L1.wnum = 224
L1.skip_cols = (96, 96)
L1.agg = 640
L1.banks = [320, 320]
L1.pw = 448
L1.sums = [(0, 0, (1, 160, 160), 0),
           (1, 160, (1, 64, 64), 160), (1, 288, (1, 96, 96), 224),
           (2, 160, (1, 64, 64), 320), (2, 256, (3, 64, 32), 384),
           (3, 160, (1, 160, 160), 480)]
L1.nhot = 4
L1.out_cols = 192
L1.kchunks = [128] * 5
L1.triples = [[("4", 1), ("4", 2), ("3", 0)], [("4", 0), ("4", 2), ("3", 1)], [("3", 2), ("4", 0), ("4", 1)]]


def turns(eng, steps, slots, body, tail=0):
    assert steps % slots == 0
    for it in range(2):
        for s in range(slots):
            body(it * slots + s, it, s)
    with eng.Fori(2, steps // slots) as it:
        for s in range(slots):
            body(None, it, s)
    for s in range(tail):
        body(steps + s, steps // slots, s)


class Shared:
    pass


def build(nc, t, out):
    est = ExitStack()
    g = Shared()
    with est:
        def sb(name, shape, dt, ctx=est):
            return ctx.enter_context(nc.sbuf_tensor(name, shape, dt))

        def sem(name, ctx=est):
            return ctx.enter_context(nc.semaphore(name))

        def dram(name, shape, dt):
            return nc.dram_tensor(name, shape, dt, kind="Internal").ap()

        g.ps = [est.enter_context(nc.psum_tensor(f"bank{i}", [P, 512], F32)) for i in range(2)]
        g.ps2 = [est.enter_context(nc.psum_tensor(f"pair{i}", [P, 2, 512], F32)) for i in range(3)]

        g.sorted_rows = [dram(f"sorted_rows{l.n}", (E_PAD, l.width), I32) for l in (L0, L1)]
        g.feat_tab = [dram(f"feat_tab{l.n}", (N_PAD, D), F32) for l in (L0, L1)]
        g.agg_tab = [dram(f"agg_tab{l.n}", (N_TAB, l.agg), F32) for l in (L0, L1)]
        g.skip_tab = dram("skip_tab", (N_PAD, sum(L1.skip_cols)), F32)

        g.x_sb = sb("x_sb", [P, NBLK, D], F32)
        g.attr_s = sb("attr_s", [P, 3, NBLK], F32)
        g.mean_var = sb("mean_var", [P, NBLK, 2], F32)
        g.rstd = sb("rstd", [P, NBLK], F32)
        g.nmr = sb("nmr", [P, NBLK], F32)
        g.ident = sb("ident", [P, P], F32)
        g.iota_n = sb("iota_n", [P, P], F32)
        g.ones_bf = sb("ones_bf", [P, P], BF16)
        g.ones_f = sb("ones_f", [P, P], F32)
        g.after_bf = sb("after_bf", [P, P], BF16)
        g.iota_bin = sb("iota_bin", [P, NBIN], BF16)
        g.zero_bf = sb("zero_bf", [P, P], BF16)
        g.zero_wide = sb("zero_wide", [P, 4 * NBIN], BF16)
        g.before_f = sb("before_f", [P, P], F32)
        g.upto_f = sb("upto_f", [P, P], F32)
        g.w1 = [sb(f"fc1_{l.n}", [l.fc_in, 64], F32) for l in (L0, L1)]
        g.w2 = [sb(f"fc2_{l.n}", [64, l.wnum], F32) for l in (L0, L1)]
        g.wn_s = [sb(f"node_s{l.n}", [S0, S0 + l.skip_cols[0]], F32) for l in (L0, L1)]
        g.wn_v = [sb(f"node_v{l.n}", [V0, V0 + l.skip_cols[1]], F32) for l in (L0, L1)]
        g.w_out = [sb(f"w_out{l.n}", [P, len(l.kchunks), l.out_cols], F32) for l in (L0, L1)]
        g.neg_cross = sb("neg_cross", [32, 32], F32)
        g.first_row = [sb(f"first_row{l.n}", [1, NST], I32) for l in (L0, L1)]
        g.block_of = [sb(f"block_of{l.n}", [1, NST], I32) for l in (L0, L1)]
        g.is_last = [sb(f"is_last{l.n}", [1, NST], I32) for l in (L0, L1)]
        g.base_node = [sb(f"base_node{l.n}", [P, NST], F32) for l in (L0, L1)]
        g.same_block = [sb(f"same_block{l.n}", [P, NST], F32) for l in (L0, L1)]
        g.bin_start = [sb(f"bin_start{l.n}", [1, NBIN], F32) for l in (L0, L1)]
        g.hi = [sb(f"hi{l.n}", [P, NCOL], BF16) for l in (L0, L1)]

        g.passed = sem("passed")
        setup(nc, t, g)
        for l in (L0, L1):
            count_bins(nc, l, g)
        rank_and_scatter(nc, t, L0, g)
        rank_and_scatter(nc, t, L1, g)
        node_features(nc, L0, g)
        messages(nc, L0, g)
        node_sums0(nc, g)
        node_features(nc, L1, g)
        messages(nc, L1, g)
        node_sums1(nc, out, g)


def settle(eng, passed):
    eng.sem_inc(passed, 1)


def setup(nc, t, g):
    with ExitStack() as ctx:
        s_zero = ctx.enter_context(nc.semaphore("s_zero"))
        s_const = ctx.enter_context(nc.semaphore("s_const"))
        s_in = ctx.enter_context(nc.semaphore("s_in"))
        s_keys = ctx.enter_context(nc.semaphore("s_keys"))
        s_w = ctx.enter_context(nc.semaphore("s_w"))
        s_wz = ctx.enter_context(nc.semaphore("s_wz"))
        s_neg = ctx.enter_context(nc.semaphore("s_neg"))
        s_tail = ctx.enter_context(nc.semaphore("s_tail"))
        s_shift = ctx.enter_context(nc.semaphore("s_shift"))
        s_dve = ctx.enter_context(nc.semaphore("s_dve"))
        keys = [ctx.enter_context(nc.sbuf_tensor(f"keys{n}", [P, NCOL], I32)) for n in range(2)]
        blocks = [ctx.enter_context(nc.sbuf_tensor(f"blocks{n}", [P, NCOL], I32)) for n in range(2)]
        attr = ctx.enter_context(nc.sbuf_tensor("attr", [P, NBLK], F32))
        block = ctx.enter_context(nc.Block())

        placed = []

        def rows_into(l, row, src, col):
            n, done = src.shape[0], 0
            while done < n:
                r = row + done
                k = min(n - done, P - r % P)
                placed.append((g.w_out[l.n][r % P:r % P + k, r // P, col:col + src.shape[1]], src[done:done + k, :]))
                done += k

        rows_into(L0, 96, t["L0_gnn_Wl2_s"][0:64, :], 0)
        rows_into(L0, 96, t["L0_gnn_Wa"][0:64, :], 160)
        for m in range(3):
            rows_into(L0, 32 * m, t["L0_gnn_Wl2_v"][64:96, :], 64 + 32 * m)
            rows_into(L0, 160 + 96 * m, t["L0_gnn_Wl2_v"][0:64, :], 64 + 32 * m)
            rows_into(L0, 224 + 96 * m, t["L0_gnn_Wl2_s"][64:96, :], 0)
            rows_into(L0, 224 + 96 * m, t["L0_gnn_Wa"][64:96, :], 160)
        rows_into(L1, 96, t["L1_gnn_W_out_s"][0:64, :], 0)
        for k in range(3):
            rows_into(L1, 32 * k, t["L1_gnn_W_out_v"][64:96, :], 96 + 32 * k)
            rows_into(L1, 160 * (k + 1), t["L1_gnn_W_out_v"][0:64, :], 96 + 32 * k)
            for q, (what, j) in enumerate(L1.triples[k]):
                row = 160 * (k + 1) + 64 + 32 * q
                if what == "3":
                    rows_into(L1, row, t["L1_gnn_W_out_s"][64:96, :], 0)
                else:
                    i = 3 - j - k
                    plus = (i, j, k) in ((0, 1, 2), (1, 2, 0), (2, 0, 1))
                    rows_into(L1, row, t["L1_gnn_W_out_v"][96:128, :] if plus else g.neg_cross[:, :], 96 + 32 * i)
        for l, (feat, skip) in ((L0, ("L0_gnn_Wl1_1", "L0_gnn_Wsc1")), (L1, ("L1_gnn_W_nl1", "L1_gnn_W_skip1"))):
            for m in range(3):
                placed.append((g.wn_v[l.n][m:V0:3, 32 * m:32 * m + 32], t[feat]))
                placed.append((g.wn_v[l.n][m:V0:3, V0 + 32 * m:V0 + 32 * m + 32], t[skip]))
        plain = [(g.w1[0][:, :], t["L0_gnn_Wfc1"]), (g.w2[0][:, :], t["L0_gnn_Wfc2"]),
                 (g.w1[1][:, :], t["L1_gnn_W_fc1"]), (g.w2[1][:, :], t["L1_gnn_W_fc2"]),
                 (g.wn_s[0][:, 0:S0], t["L0_gnn_Wl1_0"]), (g.wn_s[0][:, S0:], t["L0_gnn_Wsc0"]),
                 (g.wn_s[1][:, 0:S0], t["L1_gnn_W_nl0"]), (g.wn_s[1][:, S0:], t["L1_gnn_W_skip0"])]

        @block.sync
        def _(sp):
            for n, name in enumerate(("dst", "src")):
                sp.dma_start(keys[n][:, :], t[name]).then_inc(s_keys, 16)
            sp.dma_start(attr[:, :], t["node_vec1"]).then_inc(s_in, 16)
            sp.dma_start(g.x_sb[:, :, :], t["x"].rearrange("p (n d) -> p n d", d=D)).then_inc(s_in, 16)
            for dst, src in plain:
                sp.dma_start(dst, src).then_inc(s_w, 16)
            sp.dma_start(g.neg_cross[:, :], t["L1_gnn_W_out_v"][96:128, :]).then_inc(s_neg, 16)
            sp.wait_ge(s_wz, 4)
            sp.wait_ge(s_neg, 17)
            for dst, src in placed:
                sp.dma_start(dst, src).then_inc(s_w, 16)
            sp.wait_ge(s_w, 16 * (len(plain) + len(placed)))
            sp.wait_ge(s_in, 32)

        @block.gpsimd
        def _(pool):
            for m in (g.ident, g.before_f, g.upto_f, g.zero_bf, g.zero_wide):
                pool.memset(m[:, :], 0.0).then_inc(s_zero, 1)
            for m in (g.ones_f, g.ones_bf, g.after_bf):
                pool.memset(m[:, :], 1.0).then_inc(s_zero, 1)
            for m in g.w_out:
                pool.memset(m[:, :, :], 0.0).then_inc(s_wz, 1)
            for m in g.wn_v:
                pool.memset(m[:, :], 0.0).then_inc(s_wz, 1)
            pool.wait_ge(s_zero, 8)
            pool.iota(g.iota_n[:, :], [[1, P]], base=0, channel_multiplier=0,
                      allow_small_or_imprecise_dtypes=True).then_inc(s_const, 1)
            pool.iota(g.iota_bin[:, :], [[1, NBIN]], base=0, channel_multiplier=0,
                      allow_small_or_imprecise_dtypes=True).then_inc(s_const, 1)
            pool.affine_select(out=g.ident[:, :], in_=g.ident[:, :], compare_op=ALU.not_equal, fill=1.0,
                               base=0, pattern=[[-1, P]], channel_multiplier=1).then_inc(s_const, 1)
            pool.affine_select(out=g.before_f[:, :], in_=g.before_f[:, :], compare_op=ALU.is_ge, fill=1.0,
                               base=0, pattern=[[-1, P]], channel_multiplier=1).then_inc(s_const, 1)
            pool.affine_select(out=g.upto_f[:, :], in_=g.upto_f[:, :], compare_op=ALU.is_gt, fill=1.0,
                               base=0, pattern=[[-1, P]], channel_multiplier=1).then_inc(s_const, 1)
            pool.affine_select(out=g.after_bf[:, :], in_=g.after_bf[:, :], compare_op=ALU.is_ge, fill=0.0,
                               base=0, pattern=[[-1, P]], channel_multiplier=1).then_inc(s_const, 1)
            pool.wait_ge(s_const, 6)

        @block.vector
        def _(dve):
            dve.wait_ge(s_keys, 32)
            for n in range(2):
                dve.tensor_scalar(blocks[n][:, :], keys[n][:, :], 7, None, ALU.logical_shift_right).then_inc(s_shift, 1)
                dve.wait_ge(s_shift, 2 * n + 1)
                dve.tensor_copy(g.hi[n][:, :], blocks[n][:, :]).then_inc(s_shift, 1)
            dve.wait_ge(s_in, 32)
            for k, c in enumerate((64.0 ** -0.5, 32.0 ** -0.5, 96.0 ** -0.5)):
                dve.tensor_scalar(g.attr_s[:, k, :], attr[:, :], c, None, ALU.mult).then_inc(s_dve, 1)
            dve.wait_ge(s_w, 16 * (len(plain) + len(placed)))
            for w, a, b, c in ((g.w2[0], 0, 160, 64.0 ** -0.5), (g.w2[0], 160, 192, 64.0 ** -0.5 / SQRT3),
                               (g.w2[1], 0, 64, 1 / DENOM), (g.w2[1], 64, 128, SQRT3 / DENOM),
                               (g.w2[1], 128, 192, 1 / DENOM), (g.w2[1], 192, 224, SQRT3 * 2.0 ** -0.5 / DENOM)):
                dve.tensor_scalar(w[:, a:b], w[:, a:b], c, None, ALU.mult).then_inc(s_dve, 1)
            dve.wait_ge(s_dve, 9)

        @block.scalar
        def _(act):
            act.wait_ge(s_neg, 16)
            act.activation(g.neg_cross[:, :], g.neg_cross[:, :], ACT.Copy, scale=-1.0).then_inc(s_neg, 1)


def count_bins(nc, l, g):
    hi = g.hi[l.n]
    with ExitStack() as ctx:
        def sb(name, shape, dt):
            return ctx.enter_context(nc.sbuf_tensor(f"{name}_{l.n}", shape, dt))

        def sem(name):
            return ctx.enter_context(nc.semaphore(f"{name}_{l.n}"))

        hot = [sb(f"hot{s}", [P, CHUNK_TILES, NBIN], BF16) for s in range(2)]
        count = sb("count", [P, NBIN], F32)
        count_c = sb("count_c", [NBIN, 1], F32)
        up = sb("up", [NBLK, 1], I32)
        tiles_i = sb("tiles_i", [NBLK, 1], I32)
        tiles_c = sb("tiles_c", [NBLK, 1], F32)
        ends_c = sb("ends_c", [NBLK, 1], F32)
        count_w = sb("count_w", [NBLK, P], F32)
        tiles_w = sb("tiles_w", [NBLK, P], F32)
        iota_u = sb("iota_u", [P, NST], F32)
        done = sb("done", [NBLK, NST], F32)
        blk = sb("blk", [P, NST], F32)
        part = sb("part", [P, NST], F32)
        part2 = sb("part2", [P, NST], F32)
        part3 = sb("part3", [P, NST], F32)
        hot_ready, hot_used, counted, tab, mm, iota_ready, start_ready = (
            sem(x) for x in ("hot_ready", "hot_used", "counted", "tab", "mm", "iota_ready", "start_ready"))
        acc = g.ps[0]
        small = g.ps[1]
        block = ctx.enter_context(nc.Block())

        @block.gpsimd
        def _(pool):
            pool.iota(iota_u[:, :], [[1, NST]], base=0, channel_multiplier=0,
                      allow_small_or_imprecise_dtypes=True).then_inc(iota_ready, 1)

        @block.vector
        def _(dve):
            def one_hot(step, it, s):
                c = it * 2 + s
                if step is None or step >= 2:
                    dve.wait_ge(hot_used, c - 1)
                dve.tensor_tensor(
                    hot[s][:, :, :],
                    g.iota_bin[:, :].rearrange("p (o b) -> p o b", o=1).to_broadcast([P, CHUNK_TILES, NBIN]),
                    hi[:, bass.ds(c * CHUNK_TILES, CHUNK_TILES)].rearrange("p (k o) -> p k o", o=1)
                    .to_broadcast([P, CHUNK_TILES, NBIN]),
                    ALU.is_equal).then_inc(hot_ready, 1)
            turns(dve, NCHUNK, 2, one_hot)
            link = [0]

            def then(ins):
                link[0] += 1
                ins.then_inc(tab, 1)
                dve.wait_ge(tab, link[0])

            dve.wait_ge(counted, 1)
            then(dve.tensor_reduce(count[:, :], acc[:, 0:4 * NBIN].rearrange("p (k b) -> p b k", k=4), AX.X, ALU.add))
            dve.wait_ge(mm, 1)
            then(dve.tensor_copy(count_c[:, :], small[0:NBIN, 0:1]))
            then(dve.tensor_scalar(up[:, :], count_c[0:NBLK, :], float(ST - 1), None, ALU.add))
            then(dve.tensor_scalar(tiles_i[:, :], up[:, :], ST_SHIFT, None, ALU.logical_shift_right))
            then(dve.tensor_scalar(tiles_c[:, :], tiles_i[:, :], 1.0, None, ALU.max))
            then(dve.tensor_scalar(count_w[:, :], g.ones_f[0:NBLK, :], count_c[0:NBLK, :], None, ALU.mult))
            then(dve.tensor_scalar(tiles_w[:, :], g.ones_f[0:NBLK, :], tiles_c[:, :], None, ALU.mult))
            dve.wait_ge(mm, 2)
            dve.tensor_scalar(g.bin_start[l.n][:, :], small[0:1, 2:2 + NBIN], -1.0, None, ALU.add).then_inc(start_ready, 1)
            then(dve.tensor_copy(ends_c[:, :], small[0:NBLK, 1:2]))
            dve.wait_ge(iota_ready, 1)
            then(dve.tensor_scalar(done[:, :], iota_u[0:NBLK, :], ends_c[:, :], None, ALU.is_ge))
            dve.wait_ge(mm, 3)
            two = lambda a: a[:, :].rearrange("p (h u) -> p h u", h=2)
            then(dve.tensor_copy(two(blk), g.ps2[0][:, :, 0:HST]))
            then(dve.tensor_scalar(two(part), g.ps2[2][:, :, 0:HST], -float(ST), None, ALU.mult))
            then(dve.tensor_tensor(two(part2), g.ps2[1][:, :, 0:HST], two(part), ALU.add))
            then(dve.scalar_tensor_tensor(part3[:, :], iota_u[:, :], float(ST), part2[:, :], ALU.mult, ALU.add))
            then(dve.tensor_scalar(g.first_row[l.n][:, :], part3[0:1, :], float(E_PAD - ST), None, ALU.min))
            then(dve.tensor_copy(g.block_of[l.n][:, :], blk[0:1, :]))
            then(dve.tensor_scalar(g.base_node[l.n][:, :], blk[:, :], float(P), None, ALU.mult))
            then(dve.memset(g.same_block[l.n][:, 0:1], 0.0))
            then(dve.tensor_tensor(g.same_block[l.n][:, 1:NST], blk[:, 1:NST], blk[:, 0:NST - 1], ALU.is_equal))
            then(dve.tensor_tensor(g.is_last[l.n][:, 0:NST - 1], blk[0:1, 1:NST], blk[0:1, 0:NST - 1], ALU.not_equal))
            then(dve.memset(g.is_last[l.n][:, NST - 1:NST], 1))
            dve.wait_ge(start_ready, 1)

        @block.tensor
        def _(pe):
            pe.matmul(acc[:, 0:4 * NBIN], g.zero_bf[:, :], g.zero_wide[:, :], start=True, stop=False,
                      skip_group_check=True)

            def add(step, it, s):
                c = it * 2 + s
                pe.wait_ge(hot_ready, c + 1)
                for half in range(2):
                    mm_ = pe.matmul(acc[:, 0:4 * NBIN], g.ones_bf[:, :],
                                    hot[s][:, 4 * half:4 * half + 4, :].rearrange("p k b -> p (k b)"),
                                    start=False, stop=False, skip_group_check=True)
                mm_.then_inc(hot_used, 1)
            turns(pe, NCHUNK, 2, add)
            pe.matmul(acc[:, 0:4 * NBIN], g.zero_bf[:, :], g.zero_wide[:, :], start=False, stop=True,
                      skip_group_check=True).then_inc(counted, 1)
            pe.wait_ge(tab, 1)
            pe.matmul(small[0:NBIN, 0:1], count[0:1, :], g.ones_f[0:1, 0:1], start=True, stop=True).then_inc(mm, 1)
            pe.wait_ge(tab, 5)
            pe.matmul(small[0:NBLK, 1:2], g.upto_f[0:NBLK, 0:NBLK], tiles_c[:, :], start=True, stop=True)
            pe.matmul(small[0:1, 2:2 + NBIN], count_c[:, :], g.before_f[0:NBIN, 0:NBIN],
                      start=True, stop=True).then_inc(mm, 1)
            pe.wait_ge(tab, 9)
            for k, w in enumerate((g.ones_f[0:NBLK, :], count_w[:, :], tiles_w[:, :])):
                for h in range(2):
                    last = pe.matmul(g.ps2[k][:, h, 0:HST], w, done[:, h * HST:(h + 1) * HST], start=True, stop=True)
            last.then_inc(mm, 1)


def rank_and_scatter(nc, t, l, g):
    hi, rows_in, rows_out = g.hi[l.n], t[f"rows{l.n}"], g.sorted_rows[l.n]
    with ExitStack() as ctx:
        def sb(name, shape, dt):
            return ctx.enter_context(nc.sbuf_tensor(f"{name}_r{l.n}", shape, dt))

        def sem(name):
            return ctx.enter_context(nc.semaphore(f"{name}_r{l.n}"))

        hot = [sb(f"hot{s}", [P, CHUNK_TILES, NBIN], BF16) for s in range(2)]
        prod = [sb(f"prod{s}", [P, 2, 4 * NBIN], F32) for s in range(2)]
        base = [sb(f"base{s}", [1, NBIN], F32) for s in range(2)]
        place_all = sb("place_all", [P, NCOL], F32)
        place = [sb(f"place{s}", [P, CHUNK_TILES], I32) for s in range(SLOTS)]
        rows = [sb(f"rows{s}", [P, CHUNK_TILES, l.width], I32) for s in range(SLOTS)]
        hot_ready, total_ready, base_ready, rank_ready, prod_ready, placed, place_here = (
            sem(x) for x in ("hot_ready", "total_ready", "base_ready", "rank_ready", "prod_ready", "placed", "place_here"))
        rows_here = [sem(f"rows_here{s}") for s in range(SLOTS)]
        rows_sent = [sem(f"rows_sent{s}") for s in range(SLOTS)]
        block = ctx.enter_context(nc.Block())

        @block.sync
        def _(sp):
            def load(step, it, s):
                c = it * SLOTS + s
                if step is None or step >= SLOTS:
                    sp.wait_ge(rows_sent[s], CHUNK_TILES * 16 * it)
                sp.dma_start(rows[s][:, :, :],
                             rows_in[bass.ds(c * CHUNK, CHUNK), :].rearrange("(p k) w -> p k w", k=CHUNK_TILES)
                             ).then_inc(rows_here[s], 16)
            turns(sp, NCHUNK, SLOTS, load)

        @block.gpsimd
        def _(pool):
            def scatter(step, it, s):
                c = it * SLOTS + s
                pool.wait_ge(placed, c + 1)
                if step is None or step >= SLOTS:
                    pool.wait_ge(rows_sent[s], CHUNK_TILES * 16 * it)
                pool.tensor_copy(place[s][:, :],
                                 place_all[:, bass.ds(c * CHUNK_TILES, CHUNK_TILES)]).then_inc(place_here, 1)
                pool.wait_ge(place_here, c + 1)
                pool.wait_ge(rows_here[s], 16 * (it + 1))
                settle(pool, g.passed)
                for k in range(CHUNK_TILES):
                    pool.indirect_dma_start(
                        out=rows_out, out_offset=bass.IndirectOffsetOnAxis(ap=place[s][:, k:k + 1], axis=0),
                        in_=rows[s][:, k, :], in_offset=None).then_inc(rows_sent[s], 16)
            turns(pool, NCHUNK, SLOTS, scatter)
            for s in range(SLOTS):
                pool.wait_ge(rows_sent[s], CHUNK_TILES * 16 * (NCHUNK // SLOTS))

        @block.vector
        def _(dve):
            dve.tensor_copy(base[0][:, :], g.bin_start[l.n][:, :]).then_inc(base_ready, 1)

            def step_(step, it, s):
                c = it * 2 + s
                if step is None or step < NCHUNK:
                    if step is None or step >= 2:
                        dve.wait_ge(rank_ready, c - 1)
                    dve.tensor_tensor(
                        hot[s][:, :, :],
                        g.iota_bin[:, :].rearrange("p (o b) -> p o b", o=1).to_broadcast([P, CHUNK_TILES, NBIN]),
                        hi[:, bass.ds(c * CHUNK_TILES, CHUNK_TILES)].rearrange("p (k o) -> p k o", o=1)
                        .to_broadcast([P, CHUNK_TILES, NBIN]),
                        ALU.is_equal).then_inc(hot_ready, 1)
                if step is None or step >= 1:
                    if step is None or step < NCHUNK:
                        dve.wait_ge(total_ready, c)
                        dve.wait_ge(base_ready, c)
                        dve.tensor_tensor(base[s][:, :], base[1 - s][:, :], g.ps[1 - s][0:1, 0:NBIN],
                                          ALU.add).then_inc(base_ready, 1)
                    dve.wait_ge(rank_ready, c)
                    dve.tensor_tensor(prod[1 - s][:, :, :], hot[1 - s][:, :, :].rearrange("p (h k) b -> p h (k b)", h=2),
                                      g.ps2[1 - s][:, :, 0:4 * NBIN], ALU.mult).then_inc(prod_ready, 1)
                    dve.wait_ge(prod_ready, c)
                    dve.tensor_reduce(place_all[:, bass.ds((c - 1) * CHUNK_TILES, CHUNK_TILES)],
                                      prod[1 - s][:, :, :].rearrange("p h (k b) -> p (h k) b", b=NBIN),
                                      AX.X, ALU.add).then_inc(placed, 1)
            turns(dve, NCHUNK, 2, step_, tail=1)

        @block.tensor
        def _(pe):
            def step_(step, it, s):
                c = it * 2 + s
                total, rank = g.ps[s][0:1, 0:NBIN], g.ps2[s]
                pe.wait_ge(hot_ready, c + 1)
                if step is None or step >= 2:
                    pe.wait_ge(base_ready, c)
                for k in range(CHUNK_TILES):
                    mm = pe.matmul(total, g.ones_bf[:, 0:1], hot[s][:, k, :], start=(k == 0),
                                   stop=(k == CHUNK_TILES - 1))
                mm.then_inc(total_ready, 1)
                if step is None or step >= 2:
                    pe.wait_ge(prod_ready, c - 1)
                for h in range(2):
                    for k in range(4 * h + 4):
                        if k >= 4 * h:
                            q = k - 4 * h
                            pe.matmul(rank[:, h, q * NBIN:(q + 1) * NBIN], g.after_bf[:, :], hot[s][:, k, :],
                                      start=(k == 0), stop=False, skip_group_check=True)
                        f = max(k + 1 - 4 * h, 0)
                        if f < 4:
                            pe.matmul(rank[:, h, f * NBIN:4 * NBIN].rearrange("p (n b) -> p n b", b=NBIN),
                                      g.ones_bf[:, :],
                                      hot[s][:, k:k + 1, :].to_broadcast([P, 4 - f, NBIN]),
                                      start=(h > 0 and k == 0), stop=False, skip_group_check=True)
                pe.wait_ge(base_ready, c + 1)
                for h in range(2):
                    mm = pe.matmul(rank[:, h, 0:4 * NBIN].rearrange("p (n b) -> p n b", b=NBIN), g.ones_f[0:1, :],
                                   base[s][:, :].rearrange("p (o b) -> p o b", o=1).to_broadcast([1, 4, NBIN]),
                                   start=False, stop=True, skip_group_check=True)
                mm.then_inc(rank_ready, 1)
            turns(pe, NCHUNK, 2, step_)


def node_features(nc, l, g):
    with ExitStack() as ctx:
        def sb(name, shape, dt):
            return ctx.enter_context(nc.sbuf_tensor(f"{name}_f{l.n}", shape, dt))

        def sem(name):
            return ctx.enter_context(nc.semaphore(f"{name}_f{l.n}"))

        stats = [sb(f"stats{s}", [P, 6], F32) for s in range(2)]
        mv = [sb(f"mv{s}", [P, 2], F32) for s in range(2)]
        eps = sb("eps", [P, 1], F32)
        std = sb("std", [P, NBLK], F32)
        h = [sb(f"h{s}", [P, D], F32) for s in range(2)]
        hT = [sb(f"hT{s}", [P, 2, P], F32) for s in range(2)]
        nskip = sum(l.skip_cols)
        feat = [sb(f"feat{s}", [P, D], F32) for s in range(2)]
        skip = [sb(f"skip{s}", [P, nskip], F32) for s in range(2)]
        ln = sem("ln")
        norm, root = sem("norm"), sem("root")
        h_ready, t_ready, hT_ready, mm_ready, feat_ready = (
            sem(x) for x in ("h_ready", "t_ready", "hT_ready", "mm_ready", "feat_ready"))
        stored = [sem(f"stored{s}") for s in range(2)]
        per = 16 * (1 + l.n)
        ns = S0 + l.skip_cols[0]
        nv = V0 + l.skip_cols[1]
        block = ctx.enter_context(nc.Block())

        @block.vector
        def _(dve):
            dve.memset(eps[:, :], LN_EPS).then_inc(norm, 1)

            def stat(step, it, s):
                b = it * 2 + s
                dve.bn_stats(stats[s][:, :], g.x_sb[:, bass.ds(b, 1), :].rearrange("p o d -> p (o d)")).then_inc(ln, 1)
                dve.wait_ge(ln, 3 * b + 1)
                settle(dve, g.passed)
                dve.bn_aggr(mv[s][:, :], stats[s][:, :]).then_inc(ln, 1)
                dve.wait_ge(ln, 3 * b + 2)
                dve.tensor_copy(g.mean_var[:, bass.ds(b, 1), :].rearrange("p o d -> p (o d)"), mv[s][:, :]).then_inc(ln, 1)
            turns(dve, NBLK, 2, stat)
            dve.wait_ge(ln, 3 * NBLK)
            dve.wait_ge(root, 1)
            dve.reciprocal(g.rstd[:, :], std[:, :]).then_inc(norm, 1)
            dve.wait_ge(norm, 2)
            dve.scalar_tensor_tensor(g.nmr[:, :], g.mean_var[:, :, 0], -1.0, g.rstd[:, :],
                                     ALU.mult, ALU.mult).then_inc(norm, 1)

            def move(step, it, s):
                b = it * 2 + s
                dve.wait_ge(t_ready, b + 1)
                if step is None or step >= 2:
                    dve.wait_ge(mm_ready, b - 1)
                dve.tensor_copy(hT[s][0:S0, 0, :], g.ps[s][0:S0, 0:P])
                dve.tensor_copy(hT[s][0:V0, 1, :], g.ps[s][0:V0, P:2 * P]).then_inc(hT_ready, 1)

            def finish(step, it, s):
                b = it * 2 + s
                res = g.ps2[s]
                dve.wait_ge(mm_ready, b + 1)
                if step is None or step >= 2:
                    dve.wait_ge(stored[s], per * it)
                if l.n == 0:
                    a8, a32 = (g.attr_s[:, k, bass.ds(b, 1)] for k in (0, 1))
                    xs = g.x_sb[:, bass.ds(b, 1), 0:S0].rearrange("p o d -> p (o d)")
                    xv = g.x_sb[:, bass.ds(b, 1), S0:D].rearrange("p o (v m) -> p (o m) v", m=3)
                    dve.tensor_scalar(feat[s][:, 0:S0], res[:, 0, 0:S0], a8, None, ALU.mult)
                    dve.tensor_scalar(feat[s][:, S0:D], res[:, 1, 0:V0], a32, None, ALU.mult)
                    dve.scalar_tensor_tensor(xs, res[:, 0, S0:ns], a8, xs, ALU.mult, ALU.add)
                    dve.scalar_tensor_tensor(xv, res[:, 1, V0:nv].rearrange("p (m v) -> p m v", m=3), a32, xv,
                                             ALU.mult, ALU.add).then_inc(feat_ready, 1)
                else:
                    dve.tensor_copy(feat[s][:, 0:S0], res[:, 0, 0:S0])
                    dve.tensor_copy(feat[s][:, S0:D], res[:, 1, 0:V0])
                    dve.tensor_copy(skip[s][:, 0:l.skip_cols[0]], res[:, 0, S0:ns])
                    dve.tensor_copy(skip[s][:, l.skip_cols[0]:], res[:, 1, V0:nv]).then_inc(feat_ready, 1)

            def step_(step, it, s):
                if step is None or step < NBLK:
                    move(step, it, s)
                if step is None or step >= 1:
                    q = s - 1
                    finish(None if step is None else step - 1, it if q >= 0 else it - 1, q % 2)
            turns(dve, NBLK, 2, step_, tail=1)

        @block.scalar
        def _(act):
            act.wait_ge(norm, 1)
            act.wait_ge(ln, 3 * NBLK)
            act.activation(std[:, :], g.mean_var[:, :, 1], ACT.Sqrt, bias=eps[:, :]).then_inc(root, 1)
            act.wait_ge(norm, 3)

            def relu(step, it, s):
                b = it * 2 + s
                if step is None or step >= 2:
                    act.wait_ge(t_ready, b - 1)
                act.activation(h[s][:, :], g.x_sb[:, bass.ds(b, 1), :].rearrange("p o d -> p (o d)"), ACT.Relu,
                               bias=g.nmr[:, bass.ds(b, 1)], scale=g.rstd[:, bass.ds(b, 1)]).then_inc(h_ready, 1)
            turns(act, NBLK, 2, relu)

        @block.tensor
        def _(pe):
            def trans(step, it, s):
                b = it * 2 + s
                pe.wait_ge(h_ready, b + 1)
                if step is None or step >= 2:
                    pe.wait_ge(hT_ready, b - 1)
                settle(pe, g.passed)
                pe.transpose(g.ps[s][0:S0, 0:P], h[s][:, 0:S0], g.ident[:, :])
                pe.transpose(g.ps[s][0:V0, P:2 * P], h[s][:, S0:D], g.ident[:, :]).then_inc(t_ready, 1)

            def product(step, it, s):
                b = it * 2 + s
                pe.wait_ge(hT_ready, b + 1)
                if step is None or step >= 2:
                    pe.wait_ge(feat_ready, b - 1)
                pe.matmul(g.ps2[s][:, 0, 0:ns], hT[s][0:S0, 0, :], g.wn_s[l.n][:, :], start=True, stop=True)
                pe.matmul(g.ps2[s][:, 1, 0:nv], hT[s][0:V0, 1, :], g.wn_v[l.n][:, :], start=True,
                          stop=True).then_inc(mm_ready, 1)

            def step_(step, it, s):
                if step is None or step < NBLK:
                    trans(step, it, s)
                if step is None or step >= 1:
                    q = s - 1
                    product(None if step is None else step - 1, it if q >= 0 else it - 1, q % 2)
            turns(pe, NBLK, 2, step_, tail=1)

        @block.sync
        def _(sp):
            def store(step, it, s):
                b = it * 2 + s
                sp.wait_ge(feat_ready, b + 1)
                sp.dma_start(g.feat_tab[l.n][bass.ds(b * P, P), :], feat[s][:, :]).then_inc(stored[s], 16)
                if l.n == 1:
                    sp.dma_start(g.skip_tab[bass.ds(b * P, P), :], skip[s][:, :]).then_inc(stored[s], 16)
            turns(sp, NBLK, 2, store)
            for s in range(2):
                sp.wait_ge(stored[s], per * NBLK // 2)


def messages(nc, l, g):
    nsh, sh = l.nsh, l.sh_at
    with ExitStack() as ctx:
        def sb(name, shape, dt):
            return ctx.enter_context(nc.sbuf_tensor(f"{name}_m{l.n}", shape, dt))

        def sem(name):
            return ctx.enter_context(nc.semaphore(f"{name}_m{l.n}"))

        rows = [sb(f"rows{s}", [P, ST_TILES, l.width], I32) for s in range(SLOTS)]
        feat = [sb(f"feat{s}", [P, ST_TILES, D], F32) for s in range(SLOTS)]
        key = [sb(f"key{s}", [P, ST_TILES], F32) for s in range(SLOTS)]
        hot = [sb(f"hot{s}", [P, ST_TILES, l.nhot, P], F32) for s in range(SLOTS)]
        eaT = [sb(f"eaT{s}", [l.fc_in, ST], F32) for s in range(2)]
        hT = [sb(f"hT{s}", [64, ST], F32) for s in range(2)]
        prod = [sb(f"prod{s}", [P, ST_TILES, l.pw], F32) for s in range(2)]
        acc = [sb(f"acc{s}", [P, l.agg], F32) for s in range(SLOTS)]
        sq = [sb(f"sq{s}", [P, ST_TILES, 3], F32) for s in range(2)]
        dist = [sb(f"dist{s}", [P, 3, ST_TILES], F32) for s in range(2)]
        unit = [sb(f"unit{s}", [P, ST_TILES, 3], F32) for s in range(SLOTS)]
        rows_here = [sem(f"rows_here{s}") for s in range(SLOTS)]
        feat_here = [sem(f"feat_here{s}") for s in range(SLOTS)]
        acc_stored = [sem(f"acc_stored{s}") for s in range(SLOTS)]
        (key_ready, hot_ready, hot_v, hot_a, eaT_ready, t_ready, h_ready, hT_ready, w_ready, prod_ready,
         sum_ready, acc_ready, norm, norm_root, unit_ready) = (sem(x) for x in (
             "key_ready", "hot_ready", "hot_v", "hot_a", "eaT_ready", "t_ready", "h_ready", "hT_ready", "w_ready",
             "prod_ready", "sum_ready", "acc_ready", "norm", "norm_root", "unit_ready"))
        ACT_HOTS = 2

        def stage(lag, fn):
            def run_(step, it, s):
                if step is not None and not 0 <= step - lag < NST:
                    return
                q = s - lag
                fn(None if step is None else step - lag, it + q // SLOTS if q < 0 else it, q % SLOTS)
            return run_

        def ea(s, k):
            return rows[s][:, k, :].bitcast(F32)

        block = ctx.enter_context(nc.Block())

        @block.sync
        def _(sp):
            def load(step, it, s):
                u = it * SLOTS + s
                if step is None or step >= SLOTS:
                    sp.wait_ge(t_ready, u - SLOTS + 1)
                    sp.wait_ge(hot_v, u - SLOTS + 1)
                    sp.wait_ge(hot_a, u - SLOTS + 1)
                    settle(sp, g.passed)
                    sp.wait_ge(feat_here[s], 16 * ST_TILES * it)
                    settle(sp, g.passed)
                row = sp.value_load(g.first_row[l.n][0:1, bass.ds(u, 1)], min_val=0, max_val=E_PAD - ST)
                sp.dma_start(rows[s][:, :, :],
                             g.sorted_rows[l.n][bass.ds(row, ST), :].rearrange("(p k) w -> p k w", k=ST_TILES)
                             ).then_inc(rows_here[s], 16)

            def store(step, it, s):
                u = it * SLOTS + s
                sp.wait_ge(acc_ready, u + 2)
                blk = sp.value_load(g.block_of[l.n][0:1, bass.ds(u, 1)], min_val=0, max_val=SPARE)
                last = sp.value_load(g.is_last[l.n][0:1, bass.ds(u, 1)], min_val=0, max_val=1)
                sp.dma_start(g.agg_tab[l.n][bass.ds(blk * P, P), :], acc[s][:, :],
                             cond=last).then_inc(acc_stored[s], 16)

            late = stage(SLOTS, store)

            def step_(step, it, s):
                if step is None or step < NST:
                    load(step, it, s)
                late(step, it, s)
            turns(sp, NST, SLOTS, step_, tail=SLOTS)
            for s in range(SLOTS):
                sp.wait_ge(acc_stored[s], 16 * (NST // SLOTS))

        @block.gpsimd
        def _(pool):
            def gather(step, it, s):
                u = it * SLOTS + s
                pool.wait_ge(rows_here[s], 16 * (it + 1))
                if step is None or step >= SLOTS:
                    pool.wait_ge(prod_ready, u - SLOTS + 1)
                settle(pool, g.passed)
                for k in range(ST_TILES):
                    pool.indirect_dma_start(
                        out=feat[s][:, k, :], out_offset=None, in_=g.feat_tab[l.n],
                        in_offset=bass.IndirectOffsetOnAxis(ap=rows[s][:, k, l.idx_at:l.idx_at + 1], axis=0)
                    ).then_inc(feat_here[s], 16)
            turns(pool, NST, SLOTS, gather)

        @block.tensor
        def _(pe):
            def trans(step, it, s):
                u = it * SLOTS + s
                pe.wait_ge(rows_here[s], 16 * (it + 1))
                if step is None or step >= 2:
                    pe.wait_ge(hT_ready, u - 1)
                settle(pe, g.passed)
                for k in range(ST_TILES):
                    mm = pe.transpose(g.ps[s % 2][0:l.fc_in, k * P:(k + 1) * P], ea(s, k)[:, 0:l.fc_in], g.ident[:, :])
                mm.then_inc(t_ready, 1)

            def hidden(step, it, s):
                u = it * SLOTS + s
                pe.wait_ge(eaT_ready, u + 1)
                settle(pe, g.passed)
                pe.matmul(g.ps[s % 2][0:64, ST:2 * ST], g.w1[l.n][:, :], eaT[s % 2][:, :], start=True,
                          stop=True).then_inc(h_ready, 1)

            def weights(step, it, s):
                u = it * SLOTS + s
                pe.wait_ge(hT_ready, u + 1)
                if step is None or step >= 2:
                    pe.wait_ge(prod_ready, u - 1)
                for k in range(ST_TILES):
                    mm = pe.matmul(g.ps2[0][:, s % 2, k * l.wnum:(k + 1) * l.wnum], hT[s % 2][:, k * P:(k + 1) * P],
                                   g.w2[l.n][:, :], start=True, stop=True)
                mm.then_inc(w_ready, 1)

            def sums(step, it, s):
                u = it * SLOTS + s
                res = g.ps2[1 + s % 2]
                pe.wait_ge(hot_v, u + 1)
                pe.wait_ge(hot_a, u + 1)
                pe.wait_ge(prod_ready, u + 1)
                if step is None or step >= 2:
                    pe.wait_ge(acc_ready, u)
                opened = set()
                for k in range(ST_TILES):
                    plan = list(l.sums)
                    if l.n == 0:
                        plan.append((0, None, (1, 1, 1), 448))
                    for hot_n, p0, (n, step_w, w), col in plan:
                        bank, col = (0, col) if len(l.banks) == 1 else (col // 320, col % 320)
                        dst = res[:, bank, col:col + n * w]
                        if p0 is None:
                            rhs = g.ones_f[:, 0:1]
                        elif n == 1:
                            rhs = prod[s % 2][:, k, p0:p0 + w]
                        else:
                            rhs = prod[s % 2][:, k, p0:p0 + n * step_w].rearrange("p (n c) -> p n c", n=n)[:, :, 0:w]
                            dst = dst.rearrange("p (n c) -> p n c", n=n)
                        mm = pe.matmul(dst, hot[s][:, k, hot_n, :], rhs, start=bank not in opened,
                                       stop=(k == ST_TILES - 1), skip_group_check=True)
                        opened.add(bank)
                mm.then_inc(sum_ready, 1)

            stages = [stage(1, hidden), stage(2, weights), stage(3, sums), stage(0, trans)]

            def step_(step, it, s):
                for st in stages:
                    st(step, it, s)
            turns(pe, NST, SLOTS, step_, tail=3)

        @block.scalar
        def _(act):
            def turn_out(step, it, s):
                u = it * SLOTS + s
                act.wait_ge(t_ready, u + 1)
                if step is None or step >= 2:
                    act.wait_ge(h_ready, u - 1)
                act.activation(eaT[s % 2][:, :], g.ps[s % 2][0:l.fc_in, 0:ST], ACT.Copy).then_inc(eaT_ready, 1)

            def hidden_act(step, it, s):
                u = it * SLOTS + s
                act.wait_ge(h_ready, u + 1)
                if step is None or step >= 2:
                    act.wait_ge(w_ready, u - 1)
                act.activation(hT[s % 2][:, :], g.ps[s % 2][0:64, ST:2 * ST], ACT.Silu if l.n == 0 else ACT.Relu,
                               scale=0.25 if l.n == 0 else 1.0).then_inc(hT_ready, 1)

            def root(step, it, s):
                u = it * SLOTS + s
                act.wait_ge(norm, 2 * u + 2)
                act.activation(dist[s % 2][:, 1, :], dist[s % 2][:, 0, :], ACT.Sqrt).then_inc(norm_root, 1)

            def scale_hot(step, it, s):
                u = it * SLOTS + s
                act.wait_ge(hot_ready, u + 1)
                if l.n == 1:
                    act.wait_ge(unit_ready, u + 1)
                if step is None or step >= SLOTS:
                    act.wait_ge(sum_ready, u - SLOTS + 1)
                for k in range(ST_TILES):
                    for q in range(nsh - ACT_HOTS, nsh):
                        sc = ea(s, k)[:, sh + q:sh + q + 1] if l.n == 0 else unit[s][:, k, q:q + 1]
                        ins = act.activation(hot[s][:, k, 1 + q, :], hot[s][:, k, 0, :], ACT.Copy, scale=sc)
                ins.then_inc(hot_a, 1)

            stages = [stage(0, turn_out)] + ([stage(0, root)] if l.n == 1 else []) + [
                stage(1, hidden_act), stage(1, scale_hot)]

            def step_(step, it, s):
                for st in stages:
                    st(step, it, s)
            turns(act, NST, SLOTS, step_, tail=1)

        @block.vector
        def _(dve):
            dve.memset(acc[SLOTS - 1][:, :], 0.0).then_inc(acc_ready, 1)

            def squares(step, it, s):
                u = it * SLOTS + s
                ea3 = rows[s][:, :, sh:sh + 3].bitcast(F32)
                dve.wait_ge(rows_here[s], 16 * (it + 1))
                if step is None or step >= 2:
                    dve.wait_ge(norm_root, u - 1)
                dve.tensor_tensor(sq[s % 2][:, :, :], ea3, ea3, ALU.mult).then_inc(norm, 1)
                dve.wait_ge(norm, 2 * u + 1)
                dve.tensor_reduce(dist[s % 2][:, 0, :], sq[s % 2][:, :, :], AX.X, ALU.add).then_inc(norm, 1)

            def directions(step, it, s):
                u = it * SLOTS + s
                dve.wait_ge(norm_root, u + 1)
                dve.reciprocal(dist[s % 2][:, 2, :], dist[s % 2][:, 1, :]).then_inc(unit_ready, 1)
                dve.wait_ge(unit_ready, 2 * u + 1)
                if step is None or step >= SLOTS:
                    dve.wait_ge(hot_a, u - SLOTS + 1)
                dve.tensor_tensor(unit[s][:, :, :], rows[s][:, :, sh:sh + 3].bitcast(F32),
                                  dist[s % 2][:, 2, :].rearrange("p (k o) -> p k o", o=1)
                                  .to_broadcast([P, ST_TILES, 3]), ALU.mult).then_inc(unit_ready, 1)
                dve.wait_ge(unit_ready, 2 * u + 2)

            def one_hots(step, it, s):
                u = it * SLOTS + s
                dve.wait_ge(rows_here[s], 16 * (it + 1))
                dve.tensor_scalar(key[s][:, :], rows[s][:, :, l.key_at], g.base_node[l.n][:, bass.ds(u, 1)], None,
                                  ALU.subtract).then_inc(key_ready, 1)
                if l.n == 1:
                    directions(step, it, s)
                dve.wait_ge(key_ready, u + 1)
                if step is None or step >= SLOTS:
                    dve.wait_ge(sum_ready, u - SLOTS + 1)
                    dve.wait_ge(hot_a, u - SLOTS + 1)
                for k in range(ST_TILES):
                    ins = dve.tensor_scalar(hot[s][:, k, 0, :], g.iota_n[:, :], key[s][:, k:k + 1], None, ALU.is_equal)
                ins.then_inc(hot_ready, 1)
                dve.wait_ge(hot_ready, u + 1)
                for k in range(ST_TILES):
                    for q in range(nsh - ACT_HOTS):
                        sc = ea(s, k)[:, sh + q:sh + q + 1] if l.n == 0 else unit[s][:, k, q:q + 1]
                        ins = dve.tensor_scalar(hot[s][:, k, 1 + q, :], hot[s][:, k, 0, :], sc, None, ALU.mult)
                ins.then_inc(hot_v, 1)

            def products(step, it, s):
                u = it * SLOTS + s
                w = g.ps2[0][:, s % 2, 0:ST_TILES * l.wnum].rearrange("p (k c) -> p k c", k=ST_TILES)
                out_p = prod[s % 2]
                dve.wait_ge(w_ready, u + 1)
                dve.wait_ge(feat_here[s], 16 * ST_TILES * (it + 1))
                if step is None or step >= 2:
                    dve.wait_ge(sum_ready, u - 1)
                dve.tensor_tensor(out_p[:, :, 96:224].rearrange("p k (t c) -> p k t c", t=2),
                                  w[:, :, 0:128].rearrange("p k (t c) -> p k t c", t=2),
                                  feat[s][:, :, 0:S0].rearrange("p k (o c) -> p k o c", o=1)
                                  .to_broadcast([P, ST_TILES, 2, S0]), ALU.mult)

                def vectors(wcol, pcol, m0, m1):
                    n = m1 - m0
                    return dve.tensor_tensor(
                        out_p[:, :, pcol:pcol + 32 * n].rearrange("p k (m c) -> p k m c", m=n),
                        w[:, :, wcol:wcol + 32].rearrange("p k (o c) -> p k o c", o=1).to_broadcast([P, ST_TILES, n, 32]),
                        feat[s][:, :, S0 + 32 * m0:S0 + 32 * m1].rearrange("p k (m c) -> p k m c", m=n), ALU.mult)
                vectors(128, 0, 0, 3)
                if l.n == 0:
                    vectors(160, 224, 0, 3).then_inc(prod_ready, 1)
                else:
                    vectors(192, 256, 0, 3)
                    vectors(160, 352, 0, 2)
                    vectors(160, 224, 2, 3).then_inc(prod_ready, 1)

            def add_up(step, it, s):
                u = it * SLOTS + s
                dve.wait_ge(sum_ready, u + 1)
                dve.wait_ge(acc_ready, u + 1)
                if step is None or step >= SLOTS:
                    dve.wait_ge(acc_stored[s], 16 * it)
                prev, same = acc[(s - 1) % SLOTS], g.same_block[l.n][:, bass.ds(u, 1)]
                if l.n == 0:
                    dve.scalar_tensor_tensor(acc[s][:, :], prev[:, :], same, g.ps2[1 + s % 2][:, 0, 0:l.agg],
                                             ALU.mult, ALU.add).then_inc(acc_ready, 1)
                else:
                    half = lambda a: a[:, :].rearrange("p (h c) -> p h c", h=2)
                    dve.scalar_tensor_tensor(half(acc[s]), half(prev), same, g.ps2[1 + s % 2][:, :, 0:320],
                                             ALU.mult, ALU.add).then_inc(acc_ready, 1)

            stages = ([stage(0, squares)] if l.n == 1 else []) + [stage(1, one_hots), stage(2, products), stage(3, add_up)]

            def step_(step, it, s):
                for st in stages:
                    st(step, it, s)
            turns(dve, NST, SLOTS, step_, tail=3)


def node_sums(nc, l, g, extra):
    nk = len(l.kchunks)
    with ExitStack() as ctx:
        def sb(name, shape, dt):
            return ctx.enter_context(nc.sbuf_tensor(f"{name}_s{l.n}", shape, dt))

        def sem(name):
            return ctx.enter_context(nc.semaphore(f"{name}_s{l.n}"))

        e = Shared()
        e.l = l
        e.agg = [sb(f"agg{s}", [P, l.agg], F32) for s in range(2)]
        e.aggT = [sb(f"aggT{s}", [P, nk, P], F32) for s in range(2)]
        e.here = [sem(f"here{s}") for s in range(2)]
        e.t_ready, e.aT_ready, e.mm_ready, e.done = (sem(x) for x in ("t_ready", "aT_ready", "mm_ready", "done"))
        extra(e, sb, sem)
        block = ctx.enter_context(nc.Block())

        @block.sync
        def _(sp):
            def step_(step, it, s):
                b = it * 2 + s
                if step is None or step < NBLK:
                    if step is None or step >= 2:
                        sp.wait_ge(e.done, b - 1)
                    sp.dma_start(e.agg[s][:, :], g.agg_tab[l.n][bass.ds(b * P, P), :]).then_inc(e.here[s], 16)
                    e.load(sp, step, it, s)
                if step is None or step >= 1:
                    q = s - 1
                    e.store(sp, None if step is None else step - 1, it if q >= 0 else it - 1, q % 2)
            turns(sp, NBLK, 2, step_, tail=1)
            e.end(sp)

        @block.tensor
        def _(pe):
            def trans(step, it, s):
                b = it * 2 + s
                pe.wait_ge(e.here[s], e.per_load * (it + 1))
                if step is None or step >= 2:
                    pe.wait_ge(e.aT_ready, b - 1)
                for k, n in enumerate(l.kchunks):
                    mm = pe.transpose(g.ps2[s][0:n, k // 4, (k % 4) * P:(k % 4 + 1) * P],
                                      e.agg[s][:, k * P:k * P + n], g.ident[:, :])
                mm.then_inc(e.t_ready, 1)

            def product(step, it, s):
                b = it * 2 + s
                pe.wait_ge(e.aT_ready, b + 1)
                if step is None or step >= 2:
                    pe.wait_ge(e.done, b - 1)
                for k, n in enumerate(l.kchunks):
                    mm = pe.matmul(g.ps[s][:, 0:l.out_cols], e.aggT[s][0:n, k, :], g.w_out[l.n][0:n, k, :],
                                   start=(k == 0), stop=(k == nk - 1))
                mm.then_inc(e.mm_ready, 1)

            def step_(step, it, s):
                if step is None or step < NBLK:
                    trans(step, it, s)
                if step is None or step >= 1:
                    q = s - 1
                    product(None if step is None else step - 1, it if q >= 0 else it - 1, q % 2)
            turns(pe, NBLK, 2, step_, tail=1)

        @block.scalar
        def _(act):
            def move(step, it, s):
                b = it * 2 + s
                act.wait_ge(e.t_ready, b + 1)
                if step is None or step >= 2:
                    act.wait_ge(e.mm_ready, b - 1)
                full = sum(n == P for n in l.kchunks)
                ins = act.activation(e.aggT[s][:, 0:min(full, 4), :],
                                     g.ps2[s][:, 0, 0:min(full, 4) * P].rearrange("p (k c) -> p k c", c=P), ACT.Copy)
                if l.n == 0:
                    ins = act.activation(e.aggT[s][0:64, 3, :], g.ps2[s][0:64, 0, 3 * P:4 * P], ACT.Copy)
                else:
                    ins = act.activation(e.aggT[s][:, 4, :], g.ps2[s][:, 1, 0:P], ACT.Copy)
                ins.then_inc(e.aT_ready, 1)

            def step_(step, it, s):
                if step is None or step >= 2:
                    e.act(act, None if step is None else step - 2, it - 1, s)
                if step is None or step < NBLK:
                    move(step, it, s)
            turns(act, NBLK, 2, step_, tail=2)

        @block.vector
        def _(dve):
            def step_(step, it, s):
                if step is None or step >= 2:
                    e.finish(dve, None if step is None else step - 2, it - 1, s)
            turns(dve, NBLK, 2, step_, tail=2)


def node_sums0(nc, g):

    def extra(e, sb, sem):
        e.per_load = 16
        cnt = [sb(f"cnt{s}", [P, 4], F32) for s in range(2)]
        chain = sem("chain")
        e.load = lambda *a: None
        e.store = lambda *a: None
        e.act = lambda *a: None
        e.end = lambda sp: None

        def finish(dve, step, it, s):
            b = it * 2 + s
            c, res = cnt[s], g.ps[s]
            dve.wait_ge(e.here[s], 16 * (it + 1))
            dve.tensor_scalar(c[:, 0:1], e.agg[s][:, 448:449], 1.0, None, ALU.max).then_inc(chain, 1)
            dve.wait_ge(chain, 4 * b + 1)
            dve.reciprocal(c[:, 1:2], c[:, 0:1]).then_inc(chain, 1)
            dve.wait_ge(chain, 4 * b + 2)
            dve.tensor_tensor(c[:, 2:3], c[:, 1:2], g.attr_s[:, 2, bass.ds(b, 1)], ALU.mult).then_inc(chain, 1)
            dve.wait_ge(chain, 4 * b + 3)
            dve.wait_ge(e.mm_ready, b + 1)
            dve.tensor_scalar(c[:, 3:4], res[:, 160:161], c[:, 2:3], c[:, 2:3], ALU.mult, ALU.mult).then_inc(chain, 1)
            dve.wait_ge(chain, 4 * b + 4)
            xs = g.x_sb[:, bass.ds(b, 1), 0:S0].rearrange("p o d -> p (o d)")
            xv = g.x_sb[:, bass.ds(b, 1), S0:D].rearrange("p o (v m) -> p (o m) v", m=3)
            dve.scalar_tensor_tensor(xs, res[:, 0:S0], c[:, 3:4], xs, ALU.mult, ALU.add)
            dve.scalar_tensor_tensor(xv, res[:, S0:D].rearrange("p (m v) -> p m v", m=3), c[:, 3:4], xv,
                                     ALU.mult, ALU.add).then_inc(e.done, 1)
        e.finish = finish
    node_sums(nc, L0, g, extra)


def node_sums1(nc, out, g):
    l = L1

    def extra(e, sb, sem):
        e.per_load = 32
        skip = [sb(f"skip{s}", [P, 192], F32) for s in range(2)]
        pre = [sb(f"pre{s}", [P, 192], F32) for s in range(2)]
        gate = [sb(f"gate{s}", [P, 96], F32) for s in range(2)]
        res_sb = [sb(f"res{s}", [P, D], F32) for s in range(2)]
        y = [sb(f"y{s}", [P, D], F32) for s in range(2)]
        pre_ready, gate_ready, y_ready, mul_ready = (sem(x) for x in ("pre_ready", "gate_ready", "y_ready", "mul_ready"))
        stored = [sem(f"stored{s}") for s in range(2)]

        def load(sp, step, it, s):
            b = it * 2 + s
            if step is None or step >= 2:
                sp.wait_ge(pre_ready, b - 1)
            sp.dma_start(skip[s][:, :], g.skip_tab[bass.ds(b * P, P), :]).then_inc(e.here[s], 16)

        def act_part(act, step, it, s):
            b = it * 2 + s
            act.wait_ge(pre_ready, b + 1)
            if step is None or step >= 2:
                act.wait_ge(mul_ready, b - 1)
            act.activation(gate[s][:, :], pre[s][:, 0:96], ACT.Sigmoid).then_inc(gate_ready, 1)

        def finish(dve, step, it, s):
            b = it * 2 + s
            dve.wait_ge(e.mm_ready, b + 1)
            dve.wait_ge(e.here[s], 32 * (it + 1))
            if step is None or step >= 2:
                dve.wait_ge(gate_ready, b - 1)
            dve.tensor_tensor(pre[s][:, :], g.ps[s][:, 0:192], skip[s][:, :], ALU.add).then_inc(pre_ready, 1)
            dve.wait_ge(pre_ready, b + 1)
            dve.wait_ge(gate_ready, b + 1)
            dve.tensor_tensor(res_sb[s][:, 0:S0], pre[s][:, 0:S0], gate[s][:, 0:S0], ALU.mult)
            dve.tensor_tensor(res_sb[s][:, S0:D].rearrange("p (v m) -> p m v", m=3),
                              pre[s][:, 96:192].rearrange("p (m v) -> p m v", m=3),
                              gate[s][:, S0:96].rearrange("p (o v) -> p o v", o=1).to_broadcast([P, 3, 32]),
                              ALU.mult).then_inc(mul_ready, 1)
            dve.wait_ge(mul_ready, b + 1)
            if step is None or step >= 2:
                dve.wait_ge(stored[s], 16 * it)
            dve.tensor_tensor(y[s][:, :], res_sb[s][:, :], g.x_sb[:, bass.ds(b, 1), :].rearrange("p o d -> p (o d)"),
                              ALU.add).then_inc(e.done, 1)

        def store(sp, step, it, s):
            pass

        def end(sp):
            for s in range(2):
                sp.wait_ge(stored[s], 16 * NBLK // 2)

        e.load, e.act, e.finish, e.end = load, act_part, finish, end

        def store(sp, step, it, s):
            b = it * 2 + s
            sp.wait_ge(e.done, b + 1)
            sp.dma_start(out[bass.ds(b * P, P), :], y[s][:, :]).then_inc(stored[s], 16)
        e.store = store
    node_sums(nc, L1, g, extra)


WEIGHTS = ["L0_gnn_Wfc1", "L0_gnn_Wfc2", "L0_gnn_Wsc0", "L0_gnn_Wsc1", "L0_gnn_Wl1_0", "L0_gnn_Wl1_1", "L0_gnn_Wl2_s",
           "L0_gnn_Wl2_v", "L0_gnn_Wa", "L1_gnn_W_skip0", "L1_gnn_W_skip1", "L1_gnn_W_nl0", "L1_gnn_W_nl1",
           "L1_gnn_W_fc1", "L1_gnn_W_fc2", "L1_gnn_W_out_s", "L1_gnn_W_out_v"]


def _rows(attrs, ids, pad_ids):
    n = attrs[0].shape[0]
    parts = [np.concatenate([a, np.ones((E_PAD - n, a.shape[1]), a.dtype)]).view(np.int32) for a in attrs]
    parts += [np.concatenate([i, np.full(E_PAD - n, v, i.dtype)])[:, None] for i, v in zip(ids, pad_ids)]
    return parts


def kernel(**inputs):
    import concourse.bacc as _bacc
    from concourse.bass_utils import run_bass_kernel_spmd as _run

    a = {k: np.ascontiguousarray(v) for k, v in inputs.items()}
    arrays = {k: a[k] for k in WEIGHTS}

    def by_block(v):
        v = np.concatenate([v, np.zeros((N_PAD - v.shape[0], v.shape[1]), v.dtype)])
        return np.ascontiguousarray(v.reshape(NBLK, P, -1).transpose(1, 0, 2).reshape(P, -1))

    def by_chunk(v):
        v = np.concatenate([v, np.full(E_PAD - v.shape[0], N_PAD, v.dtype)])
        return np.ascontiguousarray(v.reshape(NCHUNK, P, CHUNK_TILES).transpose(1, 0, 2).reshape(P, -1))

    arrays["x"] = by_block(a["x"])
    arrays["node_vec1"] = by_block(a["node_vec1"])
    arrays["src"] = by_chunk(a["src"])
    arrays["dst"] = by_chunk(a["dst"])
    zero = [np.zeros((E_PAD, 2), np.int32)]
    arrays["rows0"] = np.concatenate(_rows([a["edge_attr_16"], a["edge_attr_4"]], [a["src"], a["dst"]], [0, N_PAD]) + zero, axis=1)
    arrays["rows1"] = np.concatenate(_rows([a["edge_attr_64"], a["edge_attr_3"]], [a["src"], a["dst"]], [N_PAD, 0]), axis=1)

    nc = _bacc.Bacc("TRN2", target_bir_lowering=False, num_devices=1)
    t = {k: nc.dram_tensor("in_" + k, v.shape, mybir.dt.from_np(v.dtype), kind="ExternalInput").ap() for k, v in arrays.items()}
    out = nc.dram_tensor("out_x", (N_PAD, D), F32, kind="ExternalOutput").ap()
    build(nc, t, out)
    r = _run(nc, [{"in_" + k: v for k, v in arrays.items()}], core_ids=[0])
    return r.results[0]["out_x"][0:N_NODES]
```

```python
from contextlib import ExitStack

import numpy as np

import concourse.bass as bass
from concourse import mybir

F32 = mybir.dt.float32
BF16 = mybir.dt.bfloat16
I32 = mybir.dt.int32
ALU = mybir.AluOpType
ACT = mybir.ActivationFunctionType
AX = mybir.AxisListType

P = 128
N_NODES = 12500
N_EDGES = 212500
NBLK = -(-N_NODES // P)
SPARE = NBLK
N_PAD = NBLK * P
N_TAB = (NBLK + 1) * P
CHUNK_TILES = 8
CHUNK = CHUNK_TILES * P
NCHUNK = -(-N_EDGES // CHUNK)
E_PAD = NCHUNK * CHUNK
NCOL = NCHUNK * CHUNK_TILES
NBIN = 100
ST_TILES = 2
ST = ST_TILES * P
ST_SHIFT = 8
assert 1 << ST_SHIFT == ST
SLOTS = 4
AHEAD = 6
RING = 3
NST = -(-(N_EDGES // ST + NBLK) // AHEAD) * AHEAD
HST = NST // 2
LATE = NST // AHEAD
EARLY = NCHUNK - LATE
HALF = CHUNK_TILES // 2
assert E_PAD - N_EDGES >= ST and NST <= 1024 and N_TAB > N_PAD

S0, V0 = 64, 96
D = S0 + V0
SQRT3 = 3.0 ** 0.5
DENOM = 32.0
LN_EPS = 1e-5


class Layer:
    pass


L0 = Layer()
L0.n = 0
L0.fc_in, L0.ea, L0.width = 16, 20, 24
L0.sh_at, L0.nsh = 16, 4
L0.key_at, L0.idx_at = 21, 20
L0.wnum = 192
L0.skip_cols = (64, 96)
L0.agg = 481
L0.banks = [481]
L0.pw = 356
L0.ones_at, L0.p3_at, L0.p1_at = 160, 164, 228
L0.p1_rows, L0.p3_rows = (225, 321, 385), (161, 289, 449)
L0.sums = [(0, 0, (1, 161, 161), 0), (1, 164, (1, 128, 128), 161),
           (2, 196, (1, 96, 96), 289), (3, 228, (1, 96, 96), 385)]
L0.nhot = 4
L0.out_cols = 161
L0.kchunks = [128] * 4

L1 = Layer()
L1.n = 1
L1.fc_in, L1.ea, L1.width = 64, 67, 69
L1.sh_at, L1.nsh = 64, 3
L1.key_at, L1.idx_at = 67, 68
L1.wnum = 224
L1.skip_cols = (96, 96)
L1.agg = 640
L1.banks = [320, 320]
L1.pw = 448
L1.sums = [(0, 0, (1, 160, 160), 0),
           (1, 160, (1, 64, 64), 160), (1, 288, (1, 96, 96), 224),
           (2, 160, (1, 64, 64), 320), (2, 256, (3, 64, 32), 384),
           (3, 160, (1, 160, 160), 480)]
L1.nhot = 4
L1.out_cols = 192
L1.kchunks = [128] * 5
L1.triples = [[("4", 1), ("4", 2), ("3", 0)], [("4", 0), ("4", 2), ("3", 1)], [("3", 2), ("4", 0), ("4", 1)]]


def turns(eng, steps, slots, body, tail=0):
    assert steps % slots == 0
    for it in range(2):
        for s in range(slots):
            body(it * slots + s, it, s)
    with eng.Fori(2, steps // slots) as it:
        for s in range(slots):
            body(None, it, s)
    for s in range(tail):
        body(steps + s, steps // slots, s)


class Shared:
    pass


def build(nc, t, out):
    est = ExitStack()
    g = Shared()
    with est:
        def sb(name, shape, dt, ctx=est):
            return ctx.enter_context(nc.sbuf_tensor(name, shape, dt))

        def sem(name, ctx=est):
            return ctx.enter_context(nc.semaphore(name))

        def dram(name, shape, dt):
            return nc.dram_tensor(name, shape, dt, kind="Internal").ap()

        g.ps = [est.enter_context(nc.psum_tensor(f"bank{i}", [P, 512], F32)) for i in range(2)]
        g.ps2 = [est.enter_context(nc.psum_tensor(f"pair{i}", [P, 2, 512], F32)) for i in range(3)]

        g.sorted_rows = [dram(f"sorted_rows{l.n}", (E_PAD, l.width), I32) for l in (L0, L1)]
        g.feat_tab = [dram(f"feat_tab{l.n}", (N_PAD, D), F32) for l in (L0, L1)]
        g.agg_tab = [dram(f"agg_tab{l.n}", (N_TAB, l.agg), F32) for l in (L0, L1)]
        g.skip_tab = dram("skip_tab", (N_PAD, sum(L1.skip_cols)), F32)

        g.x_sb = sb("x_sb", [P, NBLK, D], F32)
        g.attr_s = sb("attr_s", [P, 3, NBLK], F32)
        g.mean_var = sb("mean_var", [P, NBLK, 2], F32)
        g.rstd = sb("rstd", [P, NBLK], F32)
        g.nmr = sb("nmr", [P, NBLK], F32)
        g.ident = sb("ident", [P, P], F32)
        g.iota_n = sb("iota_n", [P, P], F32)
        g.ones_bf = sb("ones_bf", [P, P], BF16)
        g.ones_f = sb("ones_f", [P, P], F32)
        g.after_bf = sb("after_bf", [P, P], BF16)
        g.iota_bin = sb("iota_bin", [P, NBIN], BF16)
        g.zero_bf = sb("zero_bf", [P, P], BF16)
        g.zero_wide = sb("zero_wide", [P, 4 * NBIN], BF16)
        g.before_f = sb("before_f", [P, P], F32)
        g.upto_f = sb("upto_f", [P, P], F32)
        g.w1 = [sb(f"fc1_{l.n}", [l.fc_in, 64], F32) for l in (L0, L1)]
        g.w2 = [sb(f"fc2_{l.n}", [64, l.wnum], F32) for l in (L0, L1)]
        g.wn_s = [sb(f"node_s{l.n}", [S0, S0 + l.skip_cols[0]], F32) for l in (L0, L1)]
        g.wn_v = [sb(f"node_v{l.n}", [V0, V0 + l.skip_cols[1]], F32) for l in (L0, L1)]
        g.w_out = [sb(f"w_out{l.n}", [P, len(l.kchunks), l.out_cols], F32) for l in (L0, L1)]
        g.neg_cross = sb("neg_cross", [32, 32], F32)
        g.first_row = [sb(f"first_row{l.n}", [1, NST], I32) for l in (L0, L1)]
        g.block_of = [sb(f"block_of{l.n}", [1, NST], I32) for l in (L0, L1)]
        g.is_last = [sb(f"is_last{l.n}", [1, NST], I32) for l in (L0, L1)]
        g.base_node = [sb(f"base_node{l.n}", [P, NST], F32) for l in (L0, L1)]
        g.same_block = [sb(f"same_block{l.n}", [P, NST], F32) for l in (L0, L1)]
        g.bin_start = [sb(f"bin_start{l.n}", [1, NBIN], F32) for l in (L0, L1)]
        g.place_all = [sb(f"place_all{l.n}", [P, NCOL], F32) for l in (L0, L1)]
        g.hi = [sb(f"hi{l.n}", [P, NCOL], BF16) for l in (L0, L1)]

        g.passed = sem("passed")
        setup(nc, t, g)
        for l in (L0, L1):
            count_bins(nc, l, g)
        rank_and_scatter(nc, t, g)
        node_features(nc, L0, g)
        messages(nc, t, L0, g)
        node_sums0(nc, g)
        node_features(nc, L1, g)
        messages(nc, t, L1, g)
        node_sums1(nc, out, g)


def settle(eng, passed):
    eng.sem_inc(passed, 1)


def setup(nc, t, g):
    with ExitStack() as ctx:
        s_zero = ctx.enter_context(nc.semaphore("s_zero"))
        s_const = ctx.enter_context(nc.semaphore("s_const"))
        s_in = ctx.enter_context(nc.semaphore("s_in"))
        s_keys = ctx.enter_context(nc.semaphore("s_keys"))
        s_w = ctx.enter_context(nc.semaphore("s_w"))
        s_wz = ctx.enter_context(nc.semaphore("s_wz"))
        s_neg = ctx.enter_context(nc.semaphore("s_neg"))
        s_tail = ctx.enter_context(nc.semaphore("s_tail"))
        s_shift = ctx.enter_context(nc.semaphore("s_shift"))
        s_dve = ctx.enter_context(nc.semaphore("s_dve"))
        keys = [ctx.enter_context(nc.sbuf_tensor(f"keys{n}", [P, NCOL], I32)) for n in range(2)]
        blocks = [ctx.enter_context(nc.sbuf_tensor(f"blocks{n}", [P, NCOL], I32)) for n in range(2)]
        attr = ctx.enter_context(nc.sbuf_tensor("attr", [P, NBLK], F32))
        block = ctx.enter_context(nc.Block())

        placed = []

        def rows_into(l, row, src, col):
            n, done = src.shape[0], 0
            while done < n:
                r = row + done
                k = min(n - done, P - r % P)
                placed.append((g.w_out[l.n][r % P:r % P + k, r // P, col:col + src.shape[1]], src[done:done + k, :]))
                done += k

        rows_into(L0, 96, t["L0_gnn_Wl2_s"][0:64, :], 0)
        rows_into(L0, 96, t["L0_gnn_Wa"][0:64, :], 160)
        for m in range(3):
            rows_into(L0, 32 * m, t["L0_gnn_Wl2_v"][64:96, :], 64 + 32 * m)
            rows_into(L0, L0.p1_rows[m], t["L0_gnn_Wl2_v"][0:64, :], 64 + 32 * m)
            rows_into(L0, L0.p3_rows[m], t["L0_gnn_Wl2_s"][64:96, :], 0)
            rows_into(L0, L0.p3_rows[m], t["L0_gnn_Wa"][64:96, :], 160)
        rows_into(L1, 96, t["L1_gnn_W_out_s"][0:64, :], 0)
        for k in range(3):
            rows_into(L1, 32 * k, t["L1_gnn_W_out_v"][64:96, :], 96 + 32 * k)
            rows_into(L1, 160 * (k + 1), t["L1_gnn_W_out_v"][0:64, :], 96 + 32 * k)
            for q, (what, j) in enumerate(L1.triples[k]):
                row = 160 * (k + 1) + 64 + 32 * q
                if what == "3":
                    rows_into(L1, row, t["L1_gnn_W_out_s"][64:96, :], 0)
                else:
                    i = 3 - j - k
                    plus = (i, j, k) in ((0, 1, 2), (1, 2, 0), (2, 0, 1))
                    rows_into(L1, row, t["L1_gnn_W_out_v"][96:128, :] if plus else g.neg_cross[:, :], 96 + 32 * i)
        for l, (feat, skip) in ((L0, ("L0_gnn_Wl1_1", "L0_gnn_Wsc1")), (L1, ("L1_gnn_W_nl1", "L1_gnn_W_skip1"))):
            for m in range(3):
                placed.append((g.wn_v[l.n][m:V0:3, 32 * m:32 * m + 32], t[feat]))
                placed.append((g.wn_v[l.n][m:V0:3, V0 + 32 * m:V0 + 32 * m + 32], t[skip]))
        plain = [(g.w1[0][:, :], t["L0_gnn_Wfc1"]), (g.w2[0][:, :], t["L0_gnn_Wfc2"]),
                 (g.w1[1][:, :], t["L1_gnn_W_fc1"]), (g.w2[1][:, :], t["L1_gnn_W_fc2"]),
                 (g.wn_s[0][:, 0:S0], t["L0_gnn_Wl1_0"]), (g.wn_s[0][:, S0:], t["L0_gnn_Wsc0"]),
                 (g.wn_s[1][:, 0:S0], t["L1_gnn_W_nl0"]), (g.wn_s[1][:, S0:], t["L1_gnn_W_skip0"])]

        @block.sync
        def _(sp):
            for n, name in enumerate(("dst", "src")):
                sp.dma_start(keys[n][:, :], t[name]).then_inc(s_keys, 16)
            sp.dma_start(attr[:, :], t["node_vec1"]).then_inc(s_in, 16)
            sp.dma_start(g.x_sb[:, :, :], t["x"].rearrange("p (n d) -> p n d", d=D)).then_inc(s_in, 16)
            for dst, src in plain:
                sp.dma_start(dst, src).then_inc(s_w, 16)
            sp.dma_start(g.neg_cross[:, :], t["L1_gnn_W_out_v"][96:128, :]).then_inc(s_neg, 16)
            sp.wait_ge(s_wz, 4)
            sp.wait_ge(s_neg, 17)
            for dst, src in placed:
                sp.dma_start(dst, src).then_inc(s_w, 16)
            sp.wait_ge(s_w, 16 * (len(plain) + len(placed)))
            sp.wait_ge(s_in, 32)

        @block.gpsimd
        def _(pool):
            for m in (g.ident, g.before_f, g.upto_f, g.zero_bf, g.zero_wide):
                pool.memset(m[:, :], 0.0).then_inc(s_zero, 1)
            for m in (g.ones_f, g.ones_bf, g.after_bf):
                pool.memset(m[:, :], 1.0).then_inc(s_zero, 1)
            for m in g.w_out:
                pool.memset(m[:, :, :], 0.0).then_inc(s_wz, 1)
            for m in g.wn_v:
                pool.memset(m[:, :], 0.0).then_inc(s_wz, 1)
            pool.wait_ge(s_zero, 8)
            pool.iota(g.iota_n[:, :], [[1, P]], base=0, channel_multiplier=0,
                      allow_small_or_imprecise_dtypes=True).then_inc(s_const, 1)
            pool.iota(g.iota_bin[:, :], [[1, NBIN]], base=0, channel_multiplier=0,
                      allow_small_or_imprecise_dtypes=True).then_inc(s_const, 1)
            pool.affine_select(out=g.ident[:, :], in_=g.ident[:, :], compare_op=ALU.not_equal, fill=1.0,
                               base=0, pattern=[[-1, P]], channel_multiplier=1).then_inc(s_const, 1)
            pool.affine_select(out=g.before_f[:, :], in_=g.before_f[:, :], compare_op=ALU.is_ge, fill=1.0,
                               base=0, pattern=[[-1, P]], channel_multiplier=1).then_inc(s_const, 1)
            pool.affine_select(out=g.upto_f[:, :], in_=g.upto_f[:, :], compare_op=ALU.is_gt, fill=1.0,
                               base=0, pattern=[[-1, P]], channel_multiplier=1).then_inc(s_const, 1)
            pool.affine_select(out=g.after_bf[:, :], in_=g.after_bf[:, :], compare_op=ALU.is_ge, fill=0.0,
                               base=0, pattern=[[-1, P]], channel_multiplier=1).then_inc(s_const, 1)
            pool.wait_ge(s_const, 6)

        @block.vector
        def _(dve):
            dve.wait_ge(s_keys, 32)
            for n in range(2):
                dve.tensor_scalar(blocks[n][:, :], keys[n][:, :], 7, None, ALU.logical_shift_right).then_inc(s_shift, 1)
                dve.wait_ge(s_shift, 2 * n + 1)
                dve.tensor_copy(g.hi[n][:, :], blocks[n][:, :]).then_inc(s_shift, 1)
            dve.wait_ge(s_in, 32)
            for k, c in enumerate((64.0 ** -0.5, 32.0 ** -0.5, 96.0 ** -0.5)):
                dve.tensor_scalar(g.attr_s[:, k, :], attr[:, :], c, None, ALU.mult).then_inc(s_dve, 1)
            dve.wait_ge(s_w, 16 * (len(plain) + len(placed)))
            for w, a, b, c in ((g.w2[0], 0, 160, 64.0 ** -0.5), (g.w2[0], 160, 192, 64.0 ** -0.5 / SQRT3),
                               (g.w2[1], 0, 64, 1 / DENOM), (g.w2[1], 64, 128, SQRT3 / DENOM),
                               (g.w2[1], 128, 192, 1 / DENOM), (g.w2[1], 192, 224, SQRT3 * 2.0 ** -0.5 / DENOM)):
                dve.tensor_scalar(w[:, a:b], w[:, a:b], c, None, ALU.mult).then_inc(s_dve, 1)
            dve.wait_ge(s_dve, 9)

        @block.scalar
        def _(act):
            act.wait_ge(s_neg, 16)
            act.activation(g.neg_cross[:, :], g.neg_cross[:, :], ACT.Copy, scale=-1.0).then_inc(s_neg, 1)


def count_bins(nc, l, g):
    hi = g.hi[l.n]
    with ExitStack() as ctx:
        def sb(name, shape, dt):
            return ctx.enter_context(nc.sbuf_tensor(f"{name}_{l.n}", shape, dt))

        def sem(name):
            return ctx.enter_context(nc.semaphore(f"{name}_{l.n}"))

        hot = [sb(f"hot{s}", [P, CHUNK_TILES, NBIN], BF16) for s in range(2)]
        count = sb("count", [P, NBIN], F32)
        count_c = sb("count_c", [NBIN, 1], F32)
        up = sb("up", [NBLK, 1], I32)
        tiles_i = sb("tiles_i", [NBLK, 1], I32)
        tiles_c = sb("tiles_c", [NBLK, 1], F32)
        ends_c = sb("ends_c", [NBLK, 1], F32)
        count_w = sb("count_w", [NBLK, P], F32)
        tiles_w = sb("tiles_w", [NBLK, P], F32)
        iota_u = sb("iota_u", [P, NST], F32)
        done = sb("done", [NBLK, NST], F32)
        blk = sb("blk", [P, NST], F32)
        part = sb("part", [P, NST], F32)
        part2 = sb("part2", [P, NST], F32)
        part3 = sb("part3", [P, NST], F32)
        hot_ready, hot_used, counted, tab, mm, iota_ready, start_ready = (
            sem(x) for x in ("hot_ready", "hot_used", "counted", "tab", "mm", "iota_ready", "start_ready"))
        acc = g.ps[0]
        small = g.ps[1]
        block = ctx.enter_context(nc.Block())

        @block.gpsimd
        def _(pool):
            pool.iota(iota_u[:, :], [[1, NST]], base=0, channel_multiplier=0,
                      allow_small_or_imprecise_dtypes=True).then_inc(iota_ready, 1)

        @block.vector
        def _(dve):
            def one_hot(step, it, s):
                c = it * 2 + s
                if step is None or step >= 2:
                    dve.wait_ge(hot_used, c - 1)
                dve.tensor_tensor(
                    hot[s][:, :, :],
                    g.iota_bin[:, :].rearrange("p (o b) -> p o b", o=1).to_broadcast([P, CHUNK_TILES, NBIN]),
                    hi[:, bass.ds(c * CHUNK_TILES, CHUNK_TILES)].rearrange("p (k o) -> p k o", o=1)
                    .to_broadcast([P, CHUNK_TILES, NBIN]),
                    ALU.is_equal).then_inc(hot_ready, 1)
            turns(dve, NCHUNK, 2, one_hot)
            link = [0]

            def then(ins):
                link[0] += 1
                ins.then_inc(tab, 1)
                dve.wait_ge(tab, link[0])

            dve.wait_ge(counted, 1)
            then(dve.tensor_reduce(count[:, :], acc[:, 0:4 * NBIN].rearrange("p (k b) -> p b k", k=4), AX.X, ALU.add))
            dve.wait_ge(mm, 1)
            then(dve.tensor_copy(count_c[:, :], small[0:NBIN, 0:1]))
            then(dve.tensor_scalar(up[:, :], count_c[0:NBLK, :], float(ST - 1), None, ALU.add))
            then(dve.tensor_scalar(tiles_i[:, :], up[:, :], ST_SHIFT, None, ALU.logical_shift_right))
            then(dve.tensor_scalar(tiles_c[:, :], tiles_i[:, :], 1.0, None, ALU.max))
            then(dve.tensor_scalar(count_w[:, :], g.ones_f[0:NBLK, :], count_c[0:NBLK, :], None, ALU.mult))
            then(dve.tensor_scalar(tiles_w[:, :], g.ones_f[0:NBLK, :], tiles_c[:, :], None, ALU.mult))
            dve.wait_ge(mm, 2)
            dve.tensor_scalar(g.bin_start[l.n][:, :], small[0:1, 2:2 + NBIN], -1.0, None, ALU.add).then_inc(start_ready, 1)
            then(dve.tensor_copy(ends_c[:, :], small[0:NBLK, 1:2]))
            dve.wait_ge(iota_ready, 1)
            then(dve.tensor_scalar(done[:, :], iota_u[0:NBLK, :], ends_c[:, :], None, ALU.is_ge))
            dve.wait_ge(mm, 3)
            two = lambda a: a[:, :].rearrange("p (h u) -> p h u", h=2)
            then(dve.tensor_copy(two(blk), g.ps2[0][:, :, 0:HST]))
            then(dve.tensor_scalar(two(part), g.ps2[2][:, :, 0:HST], -float(ST), None, ALU.mult))
            then(dve.tensor_tensor(two(part2), g.ps2[1][:, :, 0:HST], two(part), ALU.add))
            then(dve.scalar_tensor_tensor(part3[:, :], iota_u[:, :], float(ST), part2[:, :], ALU.mult, ALU.add))
            then(dve.tensor_scalar(g.first_row[l.n][:, :], part3[0:1, :], float(E_PAD - ST), None, ALU.min))
            then(dve.tensor_copy(g.block_of[l.n][:, :], blk[0:1, :]))
            then(dve.tensor_scalar(g.base_node[l.n][:, :], blk[:, :], float(P), None, ALU.mult))
            then(dve.memset(g.same_block[l.n][:, 0:1], 0.0))
            then(dve.tensor_tensor(g.same_block[l.n][:, 1:NST], blk[:, 1:NST], blk[:, 0:NST - 1], ALU.is_equal))
            then(dve.tensor_tensor(g.is_last[l.n][:, 0:NST - 1], blk[0:1, 1:NST], blk[0:1, 0:NST - 1], ALU.not_equal))
            then(dve.memset(g.is_last[l.n][:, NST - 1:NST], 1))
            dve.wait_ge(start_ready, 1)

        @block.tensor
        def _(pe):
            pe.matmul(acc[:, 0:4 * NBIN], g.zero_bf[:, :], g.zero_wide[:, :], start=True, stop=False,
                      skip_group_check=True)

            def add(step, it, s):
                c = it * 2 + s
                pe.wait_ge(hot_ready, c + 1)
                for half in range(2):
                    mm_ = pe.matmul(acc[:, 0:4 * NBIN], g.ones_bf[:, :],
                                    hot[s][:, 4 * half:4 * half + 4, :].rearrange("p k b -> p (k b)"),
                                    start=False, stop=False, skip_group_check=True)
                mm_.then_inc(hot_used, 1)
            turns(pe, NCHUNK, 2, add)
            pe.matmul(acc[:, 0:4 * NBIN], g.zero_bf[:, :], g.zero_wide[:, :], start=False, stop=True,
                      skip_group_check=True).then_inc(counted, 1)
            pe.wait_ge(tab, 1)
            pe.matmul(small[0:NBIN, 0:1], count[0:1, :], g.ones_f[0:1, 0:1], start=True, stop=True).then_inc(mm, 1)
            pe.wait_ge(tab, 5)
            pe.matmul(small[0:NBLK, 1:2], g.upto_f[0:NBLK, 0:NBLK], tiles_c[:, :], start=True, stop=True)
            pe.matmul(small[0:1, 2:2 + NBIN], count_c[:, :], g.before_f[0:NBIN, 0:NBIN],
                      start=True, stop=True).then_inc(mm, 1)
            pe.wait_ge(tab, 9)
            for k, w in enumerate((g.ones_f[0:NBLK, :], count_w[:, :], tiles_w[:, :])):
                for h in range(2):
                    last = pe.matmul(g.ps2[k][:, h, 0:HST], w, done[:, h * HST:(h + 1) * HST], start=True, stop=True)
            last.then_inc(mm, 1)


def rank_and_scatter(nc, t, g):
    with ExitStack() as ctx:
        def buffers(l):
            def sb(name, shape, dt):
                return ctx.enter_context(nc.sbuf_tensor(f"{name}_r{l.n}", shape, dt))

            def sem(name):
                return ctx.enter_context(nc.semaphore(f"{name}_r{l.n}"))

            r = Shared()
            r.l, r.hi, r.place_all = l, g.hi[l.n], g.place_all[l.n]
            r.rows_in, r.rows_out = t[f"rows{l.n}"], g.sorted_rows[l.n]
            r.whole = (NCHUNK if l.n == 0 else EARLY) // SLOTS * SLOTS
            r.from_ = 0 if l.n == 0 else LATE
            r.more = (NCHUNK if l.n == 0 else EARLY) % SLOTS
            r.hot = [sb(f"hot{s}", [P, CHUNK_TILES, NBIN], BF16) for s in range(2)]
            r.prod = [sb(f"prod{s}", [P, 2, 4 * NBIN], F32) for s in range(2)]
            r.base = [sb(f"base{s}", [1, NBIN], F32) for s in range(2)]
            r.place = [sb(f"place{s}", [P, CHUNK_TILES], I32) for s in range(SLOTS)]
            r.rows = [sb(f"rows{s}", [P, CHUNK_TILES, l.width], I32) for s in range(SLOTS)]
            r.hot_ready, r.total_ready, r.base_ready, r.rank_ready, r.prod_ready, r.placed, r.place_here = (
                sem(x) for x in ("hot_ready", "total_ready", "base_ready", "rank_ready", "prod_ready", "placed", "place_here"))
            r.rows_here = [sem(f"rows_here{s}") for s in range(SLOTS)]
            r.rows_sent = [sem(f"rows_sent{s}") for s in range(SLOTS)]
            return r

        both = [buffers(L0), buffers(L1)]
        block = ctx.enter_context(nc.Block())

        @block.sync
        def _(sp):
            def load_rows(r):
                def load(step, it, s):
                    c = it * SLOTS + s
                    if step is None or step >= SLOTS:
                        sp.wait_ge(r.rows_sent[s], CHUNK_TILES * 16 * it)
                    sp.dma_start(r.rows[s][:, :, :],
                                 r.rows_in[bass.ds((c + r.from_) * CHUNK, CHUNK), :].rearrange("(p k) w -> p k w", k=CHUNK_TILES)
                                 ).then_inc(r.rows_here[s], 16)
                turns(sp, r.whole, SLOTS, load, tail=r.more)

            for r in both:
                load_rows(r)

        @block.gpsimd
        def _(pool):
            def scatter_rows(r):
                def scatter(step, it, s):
                    c = it * SLOTS + s
                    pool.wait_ge(r.placed, c + r.from_ + 1)
                    if step is None or step >= SLOTS:
                        pool.wait_ge(r.rows_sent[s], CHUNK_TILES * 16 * it)
                    pool.tensor_copy(r.place[s][:, :],
                                     r.place_all[:, bass.ds((c + r.from_) * CHUNK_TILES, CHUNK_TILES)]).then_inc(r.place_here, 1)
                    pool.wait_ge(r.place_here, c + 1)
                    pool.wait_ge(r.rows_here[s], 16 * (it + 1))
                    settle(pool, g.passed)
                    for k in range(CHUNK_TILES):
                        pool.indirect_dma_start(
                            out=r.rows_out, out_offset=bass.IndirectOffsetOnAxis(ap=r.place[s][:, k:k + 1], axis=0),
                            in_=r.rows[s][:, k, :], in_offset=None).then_inc(r.rows_sent[s], 16)
                turns(pool, r.whole, SLOTS, scatter, tail=r.more)
                for s in range(SLOTS):
                    pool.wait_ge(r.rows_sent[s], CHUNK_TILES * 16 * (r.whole // SLOTS + (s < r.more)))

            for r in both:
                scatter_rows(r)

        @block.vector
        def _(dve):
            def places(r):
                dve.tensor_copy(r.base[0][:, :], g.bin_start[r.l.n][:, :]).then_inc(r.base_ready, 1)

                def step_(step, it, s):
                    c = it * 2 + s
                    if step is None or step < NCHUNK:
                        if step is None or step >= 2:
                            dve.wait_ge(r.rank_ready, c - 1)
                        dve.tensor_tensor(
                            r.hot[s][:, :, :],
                            g.iota_bin[:, :].rearrange("p (o b) -> p o b", o=1).to_broadcast([P, CHUNK_TILES, NBIN]),
                            r.hi[:, bass.ds(c * CHUNK_TILES, CHUNK_TILES)].rearrange("p (k o) -> p k o", o=1)
                            .to_broadcast([P, CHUNK_TILES, NBIN]),
                            ALU.is_equal).then_inc(r.hot_ready, 1)
                    if step is None or step >= 1:
                        if step is None or step < NCHUNK:
                            dve.wait_ge(r.total_ready, c)
                            dve.wait_ge(r.base_ready, c)
                            dve.tensor_tensor(r.base[s][:, :], r.base[1 - s][:, :], g.ps[1 - s][0:1, 0:NBIN],
                                              ALU.add).then_inc(r.base_ready, 1)
                        dve.wait_ge(r.rank_ready, c)
                        dve.tensor_tensor(r.prod[1 - s][:, :, :], r.hot[1 - s][:, :, :].rearrange("p (h k) b -> p h (k b)", h=2),
                                          g.ps2[1 - s][:, :, 0:4 * NBIN], ALU.mult).then_inc(r.prod_ready, 1)
                        dve.wait_ge(r.prod_ready, c)
                        dve.tensor_reduce(r.place_all[:, bass.ds((c - 1) * CHUNK_TILES, CHUNK_TILES)],
                                          r.prod[1 - s][:, :, :].rearrange("p h (k b) -> p (h k) b", b=NBIN),
                                          AX.X, ALU.add).then_inc(r.placed, 1)
                turns(dve, NCHUNK, 2, step_, tail=1)

            for r in both:
                places(r)

        @block.tensor
        def _(pe):
            def ranks(r):
                def step_(step, it, s):
                    c = it * 2 + s
                    total, rank = g.ps[s][0:1, 0:NBIN], g.ps2[s]
                    pe.wait_ge(r.hot_ready, c + 1)
                    if step is None or step >= 2:
                        pe.wait_ge(r.base_ready, c)
                    for k in range(CHUNK_TILES):
                        mm = pe.matmul(total, g.ones_bf[:, 0:1], r.hot[s][:, k, :], start=(k == 0),
                                       stop=(k == CHUNK_TILES - 1))
                    mm.then_inc(r.total_ready, 1)
                    if step is None or step >= 2:
                        pe.wait_ge(r.prod_ready, c - 1)
                    for h in range(2):
                        for k in range(4 * h + 4):
                            if k >= 4 * h:
                                q = k - 4 * h
                                pe.matmul(rank[:, h, q * NBIN:(q + 1) * NBIN], g.after_bf[:, :], r.hot[s][:, k, :],
                                          start=(k == 0), stop=False, skip_group_check=True)
                            f = max(k + 1 - 4 * h, 0)
                            if f < 4:
                                pe.matmul(rank[:, h, f * NBIN:4 * NBIN].rearrange("p (n b) -> p n b", b=NBIN),
                                          g.ones_bf[:, :],
                                          r.hot[s][:, k:k + 1, :].to_broadcast([P, 4 - f, NBIN]),
                                          start=(h > 0 and k == 0), stop=False, skip_group_check=True)
                    pe.wait_ge(r.base_ready, c + 1)
                    for h in range(2):
                        mm = pe.matmul(rank[:, h, 0:4 * NBIN].rearrange("p (n b) -> p n b", b=NBIN), g.ones_f[0:1, :],
                                       r.base[s][:, :].rearrange("p (o b) -> p o b", o=1).to_broadcast([1, 4, NBIN]),
                                       start=False, stop=True, skip_group_check=True)
                    mm.then_inc(r.rank_ready, 1)
                turns(pe, NCHUNK, 2, step_)

            for r in both:
                if r.l.n == 1:
                    pe.wait_ge(both[0].placed, NCHUNK)
                ranks(r)


def node_features(nc, l, g):
    with ExitStack() as ctx:
        def sb(name, shape, dt):
            return ctx.enter_context(nc.sbuf_tensor(f"{name}_f{l.n}", shape, dt))

        def sem(name):
            return ctx.enter_context(nc.semaphore(f"{name}_f{l.n}"))

        stats = [sb(f"stats{s}", [P, 6], F32) for s in range(2)]
        mv = [sb(f"mv{s}", [P, 2], F32) for s in range(2)]
        eps = sb("eps", [P, 1], F32)
        std = sb("std", [P, NBLK], F32)
        h = [sb(f"h{s}", [P, D], F32) for s in range(2)]
        hT = [sb(f"hT{s}", [P, 2, P], F32) for s in range(2)]
        nskip = sum(l.skip_cols)
        feat = [sb(f"feat{s}", [P, D], F32) for s in range(2)]
        skip = [sb(f"skip{s}", [P, nskip], F32) for s in range(2)]
        ln = sem("ln")
        norm, root = sem("norm"), sem("root")
        h_ready, t_ready, hT_ready, mm_ready, feat_ready = (
            sem(x) for x in ("h_ready", "t_ready", "hT_ready", "mm_ready", "feat_ready"))
        stored = [sem(f"stored{s}") for s in range(2)]
        per = 16 * (1 + l.n)
        ns = S0 + l.skip_cols[0]
        nv = V0 + l.skip_cols[1]
        block = ctx.enter_context(nc.Block())

        @block.vector
        def _(dve):
            dve.memset(eps[:, :], LN_EPS).then_inc(norm, 1)

            def stat(step, it, s):
                b = it * 2 + s
                dve.bn_stats(stats[s][:, :], g.x_sb[:, bass.ds(b, 1), :].rearrange("p o d -> p (o d)")).then_inc(ln, 1)
                dve.wait_ge(ln, 3 * b + 1)
                settle(dve, g.passed)
                dve.bn_aggr(mv[s][:, :], stats[s][:, :]).then_inc(ln, 1)
                dve.wait_ge(ln, 3 * b + 2)
                dve.tensor_copy(g.mean_var[:, bass.ds(b, 1), :].rearrange("p o d -> p (o d)"), mv[s][:, :]).then_inc(ln, 1)
            turns(dve, NBLK, 2, stat)
            dve.wait_ge(ln, 3 * NBLK)
            dve.wait_ge(root, 1)
            dve.reciprocal(g.rstd[:, :], std[:, :]).then_inc(norm, 1)
            dve.wait_ge(norm, 2)
            dve.scalar_tensor_tensor(g.nmr[:, :], g.mean_var[:, :, 0], -1.0, g.rstd[:, :],
                                     ALU.mult, ALU.mult).then_inc(norm, 1)

            def move(step, it, s):
                b = it * 2 + s
                dve.wait_ge(t_ready, b + 1)
                if step is None or step >= 2:
                    dve.wait_ge(mm_ready, b - 1)
                dve.tensor_copy(hT[s][0:S0, 0, :], g.ps[s][0:S0, 0:P])
                dve.tensor_copy(hT[s][0:V0, 1, :], g.ps[s][0:V0, P:2 * P]).then_inc(hT_ready, 1)

            def finish(step, it, s):
                b = it * 2 + s
                res = g.ps2[s]
                dve.wait_ge(mm_ready, b + 1)
                if step is None or step >= 2:
                    dve.wait_ge(stored[s], per * it)
                if l.n == 0:
                    a8, a32 = (g.attr_s[:, k, bass.ds(b, 1)] for k in (0, 1))
                    xs = g.x_sb[:, bass.ds(b, 1), 0:S0].rearrange("p o d -> p (o d)")
                    xv = g.x_sb[:, bass.ds(b, 1), S0:D].rearrange("p o (v m) -> p (o m) v", m=3)
                    dve.tensor_scalar(feat[s][:, 0:S0], res[:, 0, 0:S0], a8, None, ALU.mult)
                    dve.tensor_scalar(feat[s][:, S0:D], res[:, 1, 0:V0], a32, None, ALU.mult)
                    dve.scalar_tensor_tensor(xs, res[:, 0, S0:ns], a8, xs, ALU.mult, ALU.add)
                    dve.scalar_tensor_tensor(xv, res[:, 1, V0:nv].rearrange("p (m v) -> p m v", m=3), a32, xv,
                                             ALU.mult, ALU.add).then_inc(feat_ready, 1)
                else:
                    dve.tensor_copy(feat[s][:, 0:S0], res[:, 0, 0:S0])
                    dve.tensor_copy(feat[s][:, S0:D], res[:, 1, 0:V0])
                    dve.tensor_copy(skip[s][:, 0:l.skip_cols[0]], res[:, 0, S0:ns])
                    dve.tensor_copy(skip[s][:, l.skip_cols[0]:], res[:, 1, V0:nv]).then_inc(feat_ready, 1)

            def step_(step, it, s):
                if step is None or step < NBLK:
                    move(step, it, s)
                if step is None or step >= 1:
                    q = s - 1
                    finish(None if step is None else step - 1, it if q >= 0 else it - 1, q % 2)
            turns(dve, NBLK, 2, step_, tail=1)

        @block.scalar
        def _(act):
            act.wait_ge(norm, 1)
            act.wait_ge(ln, 3 * NBLK)
            act.activation(std[:, :], g.mean_var[:, :, 1], ACT.Sqrt, bias=eps[:, :]).then_inc(root, 1)
            act.wait_ge(norm, 3)

            def relu(step, it, s):
                b = it * 2 + s
                if step is None or step >= 2:
                    act.wait_ge(t_ready, b - 1)
                act.activation(h[s][:, :], g.x_sb[:, bass.ds(b, 1), :].rearrange("p o d -> p (o d)"), ACT.Relu,
                               bias=g.nmr[:, bass.ds(b, 1)], scale=g.rstd[:, bass.ds(b, 1)]).then_inc(h_ready, 1)
            turns(act, NBLK, 2, relu)

        @block.tensor
        def _(pe):
            def trans(step, it, s):
                b = it * 2 + s
                pe.wait_ge(h_ready, b + 1)
                if step is None or step >= 2:
                    pe.wait_ge(hT_ready, b - 1)
                settle(pe, g.passed)
                pe.transpose(g.ps[s][0:S0, 0:P], h[s][:, 0:S0], g.ident[:, :])
                pe.transpose(g.ps[s][0:V0, P:2 * P], h[s][:, S0:D], g.ident[:, :]).then_inc(t_ready, 1)

            def product(step, it, s):
                b = it * 2 + s
                pe.wait_ge(hT_ready, b + 1)
                if step is None or step >= 2:
                    pe.wait_ge(feat_ready, b - 1)
                pe.matmul(g.ps2[s][:, 0, 0:ns], hT[s][0:S0, 0, :], g.wn_s[l.n][:, :], start=True, stop=True)
                pe.matmul(g.ps2[s][:, 1, 0:nv], hT[s][0:V0, 1, :], g.wn_v[l.n][:, :], start=True,
                          stop=True).then_inc(mm_ready, 1)

            def step_(step, it, s):
                if step is None or step < NBLK:
                    trans(step, it, s)
                if step is None or step >= 1:
                    q = s - 1
                    product(None if step is None else step - 1, it if q >= 0 else it - 1, q % 2)
            turns(pe, NBLK, 2, step_, tail=1)

        @block.sync
        def _(sp):
            def store(step, it, s):
                b = it * 2 + s
                sp.wait_ge(feat_ready, b + 1)
                sp.dma_start(g.feat_tab[l.n][bass.ds(b * P, P), :], feat[s][:, :]).then_inc(stored[s], 16)
                if l.n == 1:
                    sp.dma_start(g.skip_tab[bass.ds(b * P, P), :], skip[s][:, :]).then_inc(stored[s], 16)
            turns(sp, NBLK, 2, store)
            for s in range(2):
                sp.wait_ge(stored[s], per * NBLK // 2)


def messages(nc, t, l, g):
    nsh, sh = l.nsh, l.sh_at
    with ExitStack() as ctx:
        def sb(name, shape, dt):
            return ctx.enter_context(nc.sbuf_tensor(f"{name}_m{l.n}", shape, dt))

        def sem(name):
            return ctx.enter_context(nc.semaphore(f"{name}_m{l.n}"))

        rows = [sb(f"rows{s}", [P, ST_TILES, l.width], I32) for s in range(AHEAD)]
        feat = [sb(f"feat{s}", [P, ST_TILES, D], F32) for s in range(AHEAD)]
        key = [sb(f"key{s}", [P, ST_TILES], F32) for s in range(RING)]
        hot = [sb(f"hot{s}", [P, ST_TILES, l.nhot, P], F32) for s in range(RING)]
        eaT = [sb(f"eaT{s}", [l.fc_in, ST], F32) for s in range(2)]
        hT = [sb(f"hT{s}", [64, ST], F32) for s in range(2)]
        prod = [sb(f"prod{s}", [P, ST_TILES, l.pw], F32) for s in range(2)]
        acc = [sb(f"acc{s}", [P, l.agg], F32) for s in range(RING)]
        sq = [sb(f"sq{s}", [P, ST_TILES, 3], F32) for s in range(2)]
        dist = [sb(f"dist{s}", [P, 3, ST_TILES], F32) for s in range(2)]
        unit = [sb(f"unit{s}", [P, ST_TILES, 3], F32) for s in range(RING)]
        rows_here = [sem(f"rows_here{s}") for s in range(AHEAD)]
        feat_here = [sem(f"feat_here{s}") for s in range(AHEAD)]
        acc_stored = [sem(f"acc_stored{s}") for s in range(RING)]
        (key_ready, hot_ready, hot_v, hot_a, eaT_ready, t_ready, h_ready, hT_ready, w_ready, prod_ready,
         sum_ready, acc_ready) = (sem(x) for x in (
             "key_ready", "hot_ready", "hot_v", "hot_a", "eaT_ready", "t_ready", "h_ready", "hT_ready", "w_ready",
             "prod_ready", "sum_ready", "acc_ready"))
        if l.n == 1:
            norm, norm_root, unit_ready = (sem(x) for x in ("norm", "norm_root", "unit_ready"))
        if l.n == 0:
            later_rows = [sb(f"later_rows{h}", [P, HALF, L1.width], I32) for h in range(2)]
            later_place = [sb(f"later_place{h}", [P, HALF], I32) for h in range(2)]
            later_here = [sem(f"later_here{h}") for h in range(2)]
            later_sent = [sem(f"later_sent{h}") for h in range(2)]
            later_placed = sem("later_placed")
        ACT_HOTS = 2
        STORE_LAG = 5

        def stage(lag, fn):
            def run_(step, it, s):
                if step is not None and not 0 <= step - lag < NST:
                    return
                q = s - lag
                fn(None if step is None else step - lag, it + q // AHEAD if q < 0 else it, q % AHEAD)
            return run_

        def ea(s, k):
            return rows[s][:, k, :].bitcast(F32)

        block = ctx.enter_context(nc.Block())

        @block.sync
        def _(sp):
            def load(step, it, s):
                u = it * AHEAD + s
                if step is None or step >= AHEAD:
                    sp.wait_ge(hot_a, u - AHEAD + 1)
                    sp.wait_ge(prod_ready, u - AHEAD + 1)
                    settle(sp, g.passed)
                row = sp.value_load(g.first_row[l.n][0:1, bass.ds(u, 1)], min_val=0, max_val=E_PAD - ST)
                sp.dma_start(rows[s][:, :, :],
                             g.sorted_rows[l.n][bass.ds(row, ST), :].rearrange("(p k) w -> p k w", k=ST_TILES)
                             ).then_inc(rows_here[s], 16)

            def store(step, it, s):
                u = it * AHEAD + s
                sp.wait_ge(acc_ready, u + 2)
                settle(sp, g.passed)
                blk = sp.value_load(g.block_of[l.n][0:1, bass.ds(u, 1)], min_val=0, max_val=SPARE)
                last = sp.value_load(g.is_last[l.n][0:1, bass.ds(u, 1)], min_val=0, max_val=1)
                sp.dma_start(g.agg_tab[l.n][bass.ds(blk * P, P), :], acc[s % RING][:, :],
                             cond=last).then_inc(acc_stored[s % RING], 16)

            late = stage(STORE_LAG, store)

            def step_(step, it, s):
                if step is None or step < NST:
                    load(step, it, s)
                late(step, it, s)
            turns(sp, NST, AHEAD, step_, tail=STORE_LAG)
            for s in range(RING):
                sp.wait_ge(acc_stored[s], 16 * (NST // RING))

        @block.gpsimd
        def _(pool):
            def gather(step, it, s):
                u = it * AHEAD + s
                pool.wait_ge(rows_here[s], 16 * (it + 1))
                if step is None or step >= AHEAD:
                    pool.wait_ge(prod_ready, u - AHEAD + 1)
                settle(pool, g.passed)
                for k in range(ST_TILES):
                    pool.indirect_dma_start(
                        out=feat[s][:, k, :], out_offset=None, in_=g.feat_tab[l.n],
                        in_offset=bass.IndirectOffsetOnAxis(ap=rows[s][:, k, l.idx_at:l.idx_at + 1], axis=0)
                    ).then_inc(feat_here[s], 16)
                if l.n == 0 and s % 3 < 2:
                    scatter_two(it, s // 3, s % 3)

            def scatter_two(it, h, part):
                if part == 0:
                    pool.wait_ge(later_here[h], 16 * (it + 1))
                    settle(pool, g.passed)
                    pool.tensor_copy(later_place[h][:, :], g.place_all[1][:, bass.ds(it * CHUNK_TILES + h * HALF, HALF)]
                                     ).then_inc(later_placed, 1)
                    pool.wait_ge(later_placed, 2 * it + h + 1)
                    settle(pool, g.passed)
                for k in range(part * 2, part * 2 + 2):
                    pool.indirect_dma_start(
                        out=g.sorted_rows[1], out_offset=bass.IndirectOffsetOnAxis(ap=later_place[h][:, k:k + 1], axis=0),
                        in_=later_rows[h][:, k, :], in_offset=None).then_inc(later_sent[h], 16)

            turns(pool, NST, AHEAD, gather)
            if l.n == 0:
                for h in range(2):
                    pool.wait_ge(later_sent[h], HALF * 16 * LATE)
                    pool.wait_ge(later_here[h], 16 * (LATE + 1))

        @block.tensor
        def _(pe):
            def trans(step, it, s):
                u = it * AHEAD + s
                pe.wait_ge(rows_here[s], 16 * (it + 1))
                if step is None or step >= 2:
                    pe.wait_ge(hT_ready, u - 1)
                settle(pe, g.passed)
                for k in range(ST_TILES):
                    mm = pe.transpose(g.ps[s % 2][0:l.fc_in, k * P:(k + 1) * P], ea(s, k)[:, 0:l.fc_in], g.ident[:, :])
                mm.then_inc(t_ready, 1)

            def hidden(step, it, s):
                u = it * AHEAD + s
                pe.wait_ge(eaT_ready, u + 1)
                settle(pe, g.passed)
                pe.matmul(g.ps[s % 2][0:64, ST:2 * ST], g.w1[l.n][:, :], eaT[s % 2][:, :], start=True,
                          stop=True).then_inc(h_ready, 1)

            def weights(step, it, s):
                u = it * AHEAD + s
                pe.wait_ge(hT_ready, u + 1)
                if step is None or step >= 2:
                    pe.wait_ge(prod_ready, u - 1)
                for k in range(ST_TILES):
                    mm = pe.matmul(g.ps2[0][:, s % 2, k * l.wnum:(k + 1) * l.wnum], hT[s % 2][:, k * P:(k + 1) * P],
                                   g.w2[l.n][:, :], start=True, stop=True)
                mm.then_inc(w_ready, 1)

            def sums(step, it, s):
                u = it * AHEAD + s
                res = g.ps2[1 + s % 2]
                pe.wait_ge(hot_v, u + 1)
                pe.wait_ge(hot_a, u + 1)
                pe.wait_ge(prod_ready, u + 1)
                if step is None or step >= 2:
                    pe.wait_ge(acc_ready, u)
                opened = set()
                for k in range(ST_TILES):
                    for hot_n, p0, (n, step_w, w), col in l.sums:
                        bank, col = (0, col) if len(l.banks) == 1 else (col // 320, col % 320)
                        dst = res[:, bank, col:col + n * w]
                        if n == 1:
                            rhs = prod[s % 2][:, k, p0:p0 + w]
                        else:
                            rhs = prod[s % 2][:, k, p0:p0 + n * step_w].rearrange("p (n c) -> p n c", n=n)[:, :, 0:w]
                            dst = dst.rearrange("p (n c) -> p n c", n=n)
                        mm = pe.matmul(dst, hot[s % RING][:, k, hot_n, :], rhs, start=bank not in opened,
                                       stop=(k == ST_TILES - 1), skip_group_check=True)
                        opened.add(bank)
                mm.then_inc(sum_ready, 1)

            stages = [stage(0, trans), stage(1, hidden), stage(2, weights), stage(3, sums)]

            def step_(step, it, s):
                for st in stages:
                    st(step, it, s)
            turns(pe, NST, AHEAD, step_, tail=3)

        @block.scalar
        def _(act):
            def turn_out(step, it, s):
                u = it * AHEAD + s
                act.wait_ge(t_ready, u + 1)
                if step is None or step >= 2:
                    act.wait_ge(h_ready, u - 1)
                act.activation(eaT[s % 2][:, :], g.ps[s % 2][0:l.fc_in, 0:ST], ACT.Copy).then_inc(eaT_ready, 1)

            def hidden_act(step, it, s):
                u = it * AHEAD + s
                act.wait_ge(h_ready, u + 1)
                if step is None or step >= 2:
                    act.wait_ge(w_ready, u - 1)
                act.activation(hT[s % 2][:, :], g.ps[s % 2][0:64, ST:2 * ST], ACT.Silu if l.n == 0 else ACT.Relu,
                               scale=0.25 if l.n == 0 else 1.0).then_inc(hT_ready, 1)

            def root(step, it, s):
                u = it * AHEAD + s
                act.wait_ge(norm, 2 * u + 2)
                act.activation(dist[s % 2][:, 1, :], dist[s % 2][:, 0, :], ACT.Sqrt).then_inc(norm_root, 1)

            def scale_hot(step, it, s):
                u = it * AHEAD + s
                act.wait_ge(hot_ready, u + 1)
                if l.n == 1:
                    act.wait_ge(unit_ready, u + 1)
                if step is None or step >= RING:
                    act.wait_ge(sum_ready, u - RING + 1)
                for k in range(ST_TILES):
                    for q in range(3 - ACT_HOTS, 3):
                        sc = ea(s, k)[:, sh + 1 + q:sh + 2 + q] if l.n == 0 else unit[s % RING][:, k, q:q + 1]
                        ins = act.activation(hot[s % RING][:, k, 1 + q, :], hot[s % RING][:, k, 0, :], ACT.Copy, scale=sc)
                ins.then_inc(hot_a, 1)

            def load_half(h, chunk):
                act.dma_start(later_rows[h][:, :, :],
                              t["rows1"][bass.ds(chunk * CHUNK, CHUNK), :]
                              .rearrange("(p k) w -> p k w", k=CHUNK_TILES)[:, h * HALF:(h + 1) * HALF, :]
                              ).then_inc(later_here[h], 16)

            def load_later(step, it, s):
                if l.n == 0 and s % 3 == 2:
                    act.wait_ge(later_sent[s // 3], HALF * 16 * (it + 1))
                    settle(act, g.passed)
                    load_half(s // 3, it + 1)

            if l.n == 0:
                for h in range(2):
                    load_half(h, 0)
            stages = [stage(0, load_later), stage(0, turn_out)] + ([stage(0, root)] if l.n == 1 else []) + [
                stage(1, hidden_act), stage(1, scale_hot)]

            def step_(step, it, s):
                for st in stages:
                    st(step, it, s)
            turns(act, NST, AHEAD, step_, tail=1)

        @block.vector
        def _(dve):
            if l.n == 0:
                for s in range(2):
                    dve.memset(prod[s][:, :, l.ones_at:l.ones_at + 1], 1.0)
            dve.memset(acc[RING - 1][:, :], 0.0).then_inc(acc_ready, 1)

            def squares(step, it, s):
                u = it * AHEAD + s
                ea3 = rows[s][:, :, sh:sh + 3].bitcast(F32)
                dve.wait_ge(rows_here[s], 16 * (it + 1))
                if step is None or step >= 2:
                    dve.wait_ge(norm_root, u - 1)
                dve.tensor_tensor(sq[s % 2][:, :, :], ea3, ea3, ALU.mult).then_inc(norm, 1)
                dve.wait_ge(norm, 2 * u + 1)
                dve.tensor_reduce(dist[s % 2][:, 0, :], sq[s % 2][:, :, :], AX.X, ALU.add).then_inc(norm, 1)

            def directions(step, it, s):
                u = it * AHEAD + s
                dve.wait_ge(norm_root, u + 1)
                dve.reciprocal(dist[s % 2][:, 2, :], dist[s % 2][:, 1, :]).then_inc(unit_ready, 1)
                dve.wait_ge(unit_ready, 2 * u + 1)
                if step is None or step >= RING:
                    dve.wait_ge(hot_a, u - RING + 1)
                dve.tensor_tensor(unit[s % RING][:, :, :], rows[s][:, :, sh:sh + 3].bitcast(F32),
                                  dist[s % 2][:, 2, :].rearrange("p (k o) -> p k o", o=1)
                                  .to_broadcast([P, ST_TILES, 3]), ALU.mult).then_inc(unit_ready, 1)
                dve.wait_ge(unit_ready, 2 * u + 2)

            def one_hots(step, it, s):
                u = it * AHEAD + s
                dve.wait_ge(rows_here[s], 16 * (it + 1))
                dve.tensor_scalar(key[s % RING][:, :], rows[s][:, :, l.key_at], g.base_node[l.n][:, bass.ds(u, 1)], None,
                                  ALU.subtract).then_inc(key_ready, 1)
                if l.n == 1:
                    directions(step, it, s)
                dve.wait_ge(key_ready, u + 1)
                if step is None or step >= RING:
                    dve.wait_ge(sum_ready, u - RING + 1)
                    dve.wait_ge(hot_a, u - RING + 1)
                for k in range(ST_TILES):
                    ins = dve.tensor_scalar(hot[s % RING][:, k, 0, :], g.iota_n[:, :], key[s % RING][:, k:k + 1], None, ALU.is_equal)
                ins.then_inc(hot_ready, 1)
                dve.wait_ge(hot_ready, u + 1)
                for k in range(ST_TILES):
                    for q in range(3 - ACT_HOTS):
                        sc = ea(s, k)[:, sh + 1 + q:sh + 2 + q] if l.n == 0 else unit[s % RING][:, k, q:q + 1]
                        ins = dve.tensor_scalar(hot[s % RING][:, k, 1 + q, :], hot[s % RING][:, k, 0, :], sc, None, ALU.mult)
                ins.then_inc(hot_v, 1)

            def products(step, it, s):
                u = it * AHEAD + s
                w = g.ps2[0][:, s % 2, 0:ST_TILES * l.wnum].rearrange("p (k c) -> p k c", k=ST_TILES)
                out_p = prod[s % 2]
                dve.wait_ge(w_ready, u + 1)
                dve.wait_ge(feat_here[s], 16 * ST_TILES * (it + 1))
                if step is None or step >= 2:
                    dve.wait_ge(sum_ready, u - 1)
                def vectors(wcol, pcol, m0, m1):
                    n = m1 - m0
                    return dve.tensor_tensor(
                        out_p[:, :, pcol:pcol + 32 * n].rearrange("p k (m c) -> p k m c", m=n),
                        w[:, :, wcol:wcol + 32].rearrange("p k (o c) -> p k o c", o=1).to_broadcast([P, ST_TILES, n, 32]),
                        feat[s][:, :, S0 + 32 * m0:S0 + 32 * m1].rearrange("p k (m c) -> p k m c", m=n), ALU.mult)
                if l.n == 0:
                    for k in range(ST_TILES):
                        y0 = ea(s, k)[:, sh:sh + 1]
                        dve.scalar_tensor_tensor(out_p[:, k, 96:160], w[:, k, 0:64], y0, feat[s][:, k, 0:S0],
                                                 ALU.mult, ALU.mult)
                        three = lambda a: a.rearrange("p (m c) -> p m c", m=3)
                        dve.scalar_tensor_tensor(three(out_p[:, k, 0:96]),
                                                 w[:, k, 128:160].rearrange("p (o c) -> p o c", o=1).to_broadcast([P, 3, 32]),
                                                 y0, three(feat[s][:, k, S0:D]), ALU.mult, ALU.mult)
                    dve.tensor_tensor(out_p[:, :, l.p1_at:l.p1_at + 64], w[:, :, 64:128], feat[s][:, :, 0:S0], ALU.mult)
                    vectors(160, l.p3_at, 0, 2)
                    vectors(160, l.p1_at + 64, 2, 3).then_inc(prod_ready, 1)
                else:
                    dve.tensor_tensor(out_p[:, :, 96:224].rearrange("p k (t c) -> p k t c", t=2),
                                      w[:, :, 0:128].rearrange("p k (t c) -> p k t c", t=2),
                                      feat[s][:, :, 0:S0].rearrange("p k (o c) -> p k o c", o=1)
                                      .to_broadcast([P, ST_TILES, 2, S0]), ALU.mult)
                    vectors(128, 0, 0, 3)
                    vectors(192, 256, 0, 3)
                    vectors(160, 352, 0, 2)
                    vectors(160, 224, 2, 3).then_inc(prod_ready, 1)

            def add_up(step, it, s):
                u = it * AHEAD + s
                dve.wait_ge(sum_ready, u + 1)
                dve.wait_ge(acc_ready, u + 1)
                if step is None or step >= RING:
                    dve.wait_ge(acc_stored[s % RING], 16 * (it * (AHEAD // RING) + s // RING))
                prev, same = acc[(s - 1) % RING], g.same_block[l.n][:, bass.ds(u, 1)]
                if l.n == 0:
                    dve.scalar_tensor_tensor(acc[s % RING][:, :], prev[:, :], same, g.ps2[1 + s % 2][:, 0, 0:l.agg],
                                             ALU.mult, ALU.add).then_inc(acc_ready, 1)
                else:
                    half = lambda a: a[:, :].rearrange("p (h c) -> p h c", h=2)
                    dve.scalar_tensor_tensor(half(acc[s % RING]), half(prev), same, g.ps2[1 + s % 2][:, :, 0:320],
                                             ALU.mult, ALU.add).then_inc(acc_ready, 1)

            stages = ([stage(0, squares)] if l.n == 1 else []) + [stage(1, one_hots), stage(2, products), stage(3, add_up)]

            def step_(step, it, s):
                for st in stages:
                    st(step, it, s)
            turns(dve, NST, AHEAD, step_, tail=3)


def node_sums(nc, l, g, extra):
    nk = len(l.kchunks)
    with ExitStack() as ctx:
        def sb(name, shape, dt):
            return ctx.enter_context(nc.sbuf_tensor(f"{name}_s{l.n}", shape, dt))

        def sem(name):
            return ctx.enter_context(nc.semaphore(f"{name}_s{l.n}"))

        e = Shared()
        e.l = l
        e.agg = [sb(f"agg{s}", [P, nk * P], F32) for s in range(2)]
        e.aggT = [sb(f"aggT{s}", [P, nk, P], F32) for s in range(2)]
        e.here = [sem(f"here{s}") for s in range(2)]
        e.t_ready, e.aT_ready, e.mm_ready, e.done = (sem(x) for x in ("t_ready", "aT_ready", "mm_ready", "done"))
        if l.agg < nk * P:
            padded = sem("padded")
        extra(e, sb, sem)
        block = ctx.enter_context(nc.Block())

        @block.sync
        def _(sp):
            def step_(step, it, s):
                b = it * 2 + s
                if step is None or step < NBLK:
                    if step is None or step >= 2:
                        sp.wait_ge(e.done, b - 1)
                    sp.dma_start(e.agg[s][:, 0:l.agg], g.agg_tab[l.n][bass.ds(b * P, P), :]).then_inc(e.here[s], 16)
                    e.load(sp, step, it, s)
                if step is None or step >= 1:
                    q = s - 1
                    e.store(sp, None if step is None else step - 1, it if q >= 0 else it - 1, q % 2)
            turns(sp, NBLK, 2, step_, tail=1)
            e.end(sp)

        @block.tensor
        def _(pe):
            def trans(step, it, s):
                b = it * 2 + s
                if step is not None and l.agg < nk * P:
                    pe.wait_ge(padded, 2)
                pe.wait_ge(e.here[s], e.per_load * (it + 1))
                if step is None or step >= 2:
                    pe.wait_ge(e.aT_ready, b - 1)
                for k, n in enumerate(l.kchunks):
                    mm = pe.transpose(g.ps2[s][0:n, k // 4, (k % 4) * P:(k % 4 + 1) * P],
                                      e.agg[s][:, k * P:k * P + n], g.ident[:, :])
                mm.then_inc(e.t_ready, 1)

            def product(step, it, s):
                b = it * 2 + s
                pe.wait_ge(e.aT_ready, b + 1)
                if step is None or step >= 2:
                    pe.wait_ge(e.done, b - 1)
                for k, n in enumerate(l.kchunks):
                    mm = pe.matmul(g.ps[s][:, 0:l.out_cols], e.aggT[s][0:n, k, :], g.w_out[l.n][0:n, k, :],
                                   start=(k == 0), stop=(k == nk - 1))
                mm.then_inc(e.mm_ready, 1)

            def step_(step, it, s):
                if step is None or step < NBLK:
                    trans(step, it, s)
                if step is None or step >= 1:
                    q = s - 1
                    product(None if step is None else step - 1, it if q >= 0 else it - 1, q % 2)
            turns(pe, NBLK, 2, step_, tail=1)

        @block.scalar
        def _(act):
            def move(step, it, s):
                b = it * 2 + s
                act.wait_ge(e.t_ready, b + 1)
                if step is None or step >= 2:
                    act.wait_ge(e.mm_ready, b - 1)
                full = sum(n == P for n in l.kchunks)
                ins = act.activation(e.aggT[s][:, 0:min(full, 4), :],
                                     g.ps2[s][:, 0, 0:min(full, 4) * P].rearrange("p (k c) -> p k c", c=P), ACT.Copy)
                if l.n == 1:
                    ins = act.activation(e.aggT[s][:, 4, :], g.ps2[s][:, 1, 0:P], ACT.Copy)
                ins.then_inc(e.aT_ready, 1)

            def step_(step, it, s):
                if step is None or step >= 2:
                    e.act(act, None if step is None else step - 2, it - 1, s)
                if step is None or step < NBLK:
                    move(step, it, s)
            turns(act, NBLK, 2, step_, tail=2)

        @block.vector
        def _(dve):
            if l.agg < nk * P:
                for s in range(2):
                    dve.memset(e.agg[s][:, l.agg:nk * P], 0.0).then_inc(padded, 1)

            def step_(step, it, s):
                if step is None or step >= 2:
                    e.finish(dve, None if step is None else step - 2, it - 1, s)
            turns(dve, NBLK, 2, step_, tail=2)


def node_sums0(nc, g):

    def extra(e, sb, sem):
        e.per_load = 16
        cnt = [sb(f"cnt{s}", [P, 4], F32) for s in range(2)]
        chain = sem("chain")
        e.load = lambda *a: None
        e.store = lambda *a: None
        e.act = lambda *a: None
        e.end = lambda sp: None

        def finish(dve, step, it, s):
            b = it * 2 + s
            c, res = cnt[s], g.ps[s]
            dve.wait_ge(e.here[s], 16 * (it + 1))
            dve.tensor_scalar(c[:, 0:1], e.agg[s][:, L0.ones_at:L0.ones_at + 1], 1.0, None, ALU.max).then_inc(chain, 1)
            dve.wait_ge(chain, 4 * b + 1)
            dve.reciprocal(c[:, 1:2], c[:, 0:1]).then_inc(chain, 1)
            dve.wait_ge(chain, 4 * b + 2)
            dve.tensor_tensor(c[:, 2:3], c[:, 1:2], g.attr_s[:, 2, bass.ds(b, 1)], ALU.mult).then_inc(chain, 1)
            dve.wait_ge(chain, 4 * b + 3)
            dve.wait_ge(e.mm_ready, b + 1)
            dve.tensor_scalar(c[:, 3:4], res[:, 160:161], c[:, 2:3], c[:, 2:3], ALU.mult, ALU.mult).then_inc(chain, 1)
            dve.wait_ge(chain, 4 * b + 4)
            xs = g.x_sb[:, bass.ds(b, 1), 0:S0].rearrange("p o d -> p (o d)")
            xv = g.x_sb[:, bass.ds(b, 1), S0:D].rearrange("p o (v m) -> p (o m) v", m=3)
            dve.scalar_tensor_tensor(xs, res[:, 0:S0], c[:, 3:4], xs, ALU.mult, ALU.add)
            dve.scalar_tensor_tensor(xv, res[:, S0:D].rearrange("p (m v) -> p m v", m=3), c[:, 3:4], xv,
                                     ALU.mult, ALU.add).then_inc(e.done, 1)
        e.finish = finish
    node_sums(nc, L0, g, extra)


def node_sums1(nc, out, g):
    l = L1

    def extra(e, sb, sem):
        e.per_load = 32
        skip = [sb(f"skip{s}", [P, 192], F32) for s in range(2)]
        pre = [sb(f"pre{s}", [P, 192], F32) for s in range(2)]
        gate = [sb(f"gate{s}", [P, 96], F32) for s in range(2)]
        res_sb = [sb(f"res{s}", [P, D], F32) for s in range(2)]
        y = [sb(f"y{s}", [P, D], F32) for s in range(2)]
        pre_ready, gate_ready, mul_ready = (sem(x) for x in ("pre_ready", "gate_ready", "mul_ready"))
        stored = [sem(f"stored{s}") for s in range(2)]

        def load(sp, step, it, s):
            b = it * 2 + s
            if step is None or step >= 2:
                sp.wait_ge(pre_ready, b - 1)
            sp.dma_start(skip[s][:, :], g.skip_tab[bass.ds(b * P, P), :]).then_inc(e.here[s], 16)

        def act_part(act, step, it, s):
            b = it * 2 + s
            act.wait_ge(pre_ready, b + 1)
            if step is None or step >= 2:
                act.wait_ge(mul_ready, b - 1)
            act.activation(gate[s][:, :], pre[s][:, 0:96], ACT.Sigmoid).then_inc(gate_ready, 1)

        def finish(dve, step, it, s):
            b = it * 2 + s
            dve.wait_ge(e.mm_ready, b + 1)
            dve.wait_ge(e.here[s], 32 * (it + 1))
            if step is None or step >= 2:
                dve.wait_ge(gate_ready, b - 1)
            dve.tensor_tensor(pre[s][:, :], g.ps[s][:, 0:192], skip[s][:, :], ALU.add).then_inc(pre_ready, 1)
            dve.wait_ge(pre_ready, b + 1)
            dve.wait_ge(gate_ready, b + 1)
            dve.tensor_tensor(res_sb[s][:, 0:S0], pre[s][:, 0:S0], gate[s][:, 0:S0], ALU.mult)
            dve.tensor_tensor(res_sb[s][:, S0:D].rearrange("p (v m) -> p m v", m=3),
                              pre[s][:, 96:192].rearrange("p (m v) -> p m v", m=3),
                              gate[s][:, S0:96].rearrange("p (o v) -> p o v", o=1).to_broadcast([P, 3, 32]),
                              ALU.mult).then_inc(mul_ready, 1)
            dve.wait_ge(mul_ready, b + 1)
            if step is None or step >= 2:
                dve.wait_ge(stored[s], 16 * it)
            dve.tensor_tensor(y[s][:, :], res_sb[s][:, :], g.x_sb[:, bass.ds(b, 1), :].rearrange("p o d -> p (o d)"),
                              ALU.add).then_inc(e.done, 1)

        def store(sp, step, it, s):
            pass

        def end(sp):
            for s in range(2):
                sp.wait_ge(stored[s], 16 * NBLK // 2)

        e.load, e.act, e.finish, e.end = load, act_part, finish, end

        def store(sp, step, it, s):
            b = it * 2 + s
            sp.wait_ge(e.done, b + 1)
            sp.dma_start(out[bass.ds(b * P, P), :], y[s][:, :]).then_inc(stored[s], 16)
        e.store = store
    node_sums(nc, L1, g, extra)


WEIGHTS = ["L0_gnn_Wfc1", "L0_gnn_Wfc2", "L0_gnn_Wsc0", "L0_gnn_Wsc1", "L0_gnn_Wl1_0", "L0_gnn_Wl1_1", "L0_gnn_Wl2_s",
           "L0_gnn_Wl2_v", "L0_gnn_Wa", "L1_gnn_W_skip0", "L1_gnn_W_skip1", "L1_gnn_W_nl0", "L1_gnn_W_nl1",
           "L1_gnn_W_fc1", "L1_gnn_W_fc2", "L1_gnn_W_out_s", "L1_gnn_W_out_v"]


def _rows(attrs, ids, pad_ids):
    n = attrs[0].shape[0]
    parts = [np.concatenate([a, np.ones((E_PAD - n, a.shape[1]), a.dtype)]).view(np.int32) for a in attrs]
    parts += [np.concatenate([i, np.full(E_PAD - n, v, i.dtype)])[:, None] for i, v in zip(ids, pad_ids)]
    return parts


def kernel(**inputs):
    import concourse.bacc as _bacc
    from concourse.bass_utils import run_bass_kernel_spmd as _run

    a = {k: np.ascontiguousarray(v) for k, v in inputs.items()}
    arrays = {k: a[k] for k in WEIGHTS}

    def by_block(v):
        v = np.concatenate([v, np.zeros((N_PAD - v.shape[0], v.shape[1]), v.dtype)])
        return np.ascontiguousarray(v.reshape(NBLK, P, -1).transpose(1, 0, 2).reshape(P, -1))

    def by_chunk(v):
        v = np.concatenate([v, np.full(E_PAD - v.shape[0], N_PAD, v.dtype)])
        return np.ascontiguousarray(v.reshape(NCHUNK, P, CHUNK_TILES).transpose(1, 0, 2).reshape(P, -1))

    arrays["x"] = by_block(a["x"])
    arrays["node_vec1"] = by_block(a["node_vec1"])
    arrays["src"] = by_chunk(a["src"])
    arrays["dst"] = by_chunk(a["dst"])
    zero = [np.zeros((E_PAD, 2), np.int32)]
    arrays["rows0"] = np.concatenate(_rows([a["edge_attr_16"], a["edge_attr_4"]], [a["src"], a["dst"]], [0, N_PAD]) + zero, axis=1)
    arrays["rows1"] = np.concatenate(_rows([a["edge_attr_64"], a["edge_attr_3"]], [a["src"], a["dst"]], [N_PAD, 0]), axis=1)

    nc = _bacc.Bacc("TRN2", target_bir_lowering=False, num_devices=1)
    t = {k: nc.dram_tensor("in_" + k, v.shape, mybir.dt.from_np(v.dtype), kind="ExternalInput").ap() for k, v in arrays.items()}
    out = nc.dram_tensor("out_x", (N_PAD, D), F32, kind="ExternalOutput").ap()
    build(nc, t, out)
    r = _run(nc, [{"in_" + k: v for k, v in arrays.items()}], core_ids=[0])
    return r.results[0]["out_x"][0:N_NODES]
```
